# Optimizing a Trainium2 kernel written in Bass

```python
import numpy as np
import jax
import jax.numpy as jnp

def _softmax(x, axis=-1):
    return jax.nn.softmax(x, axis=axis)

def _gelu(x):
    return jax.nn.gelu(x, approximate=True)

def _silu(x):
    return jax.nn.silu(x)

def _sigmoid(x):
    return jax.nn.sigmoid(x)

def _layernorm(x, axis=-1, eps=1e-05):
    m = jnp.mean(x, axis=axis, keepdims=True)
    v = jnp.var(x, axis=axis, keepdims=True)
    return (x - m) / jnp.sqrt(v + eps)

def _scatter_add(tgt, idx, src, axis=0):
    return tgt.at[idx].add(src)

def _segment_sum(src, seg, n):
    return jax.ops.segment_sum(src, seg, n)
kernel_name = 'mk_seq_preln_d1_jaxref_r8_b2f98b'

def setup_inputs(seed: int=0):
    np.random.seed(seed)
    _w = jnp.asarray

    def _L0_attn_setup():
        import jax, jax.numpy as jnp
        import numpy as np
        N_HEADS = 32
        ROPE_THETA = 10000.0

        def _rope_cos_sin(sl, head_dim, dtype):
            inv_freq = 1.0 / ROPE_THETA ** (jnp.arange(0, head_dim, 2, dtype=jnp.float32) / head_dim)
            pos = jnp.arange(sl, dtype=jnp.float32)
            freqs = pos[:, None] * inv_freq[None, :]
            emb = jnp.concatenate([freqs, freqs], axis=-1)
            return (jnp.cos(emb).astype(dtype), jnp.sin(emb).astype(dtype))

        def _rotate_half(x):
            h = x.shape[-1] // 2
            return jnp.concatenate([-x[..., h:], x[..., :h]], axis=-1)
        key = jax.random.key(seed)
        ks = jax.random.split(key, 5)
        bs, sl, hs = (2, 256, 512)
        scale = hs ** (-0.5)
        return {'hidden_states': jax.random.normal(ks[0], (bs, sl, hs), jnp.float32), 'wq': jax.random.normal(ks[1], (hs, hs), jnp.float32) * scale, 'wk': jax.random.normal(ks[2], (hs, hs), jnp.float32) * scale, 'wv': jax.random.normal(ks[3], (hs, hs), jnp.float32) * scale, 'wo': jax.random.normal(ks[4], (hs, hs), jnp.float32) * scale}
    _L0_attn_in = _L0_attn_setup()

    def _L0_ffn_setup():
        import jax, jax.numpy as jnp
        import numpy as np
        import math
        B, S, IN, OUT = (4, 256, 512, 512)
        E, R, K = (8, 64, 128)
        SCALE = 64.0 / 64.0
        MULTIPLIER = 1.0
        key = jax.random.key(seed)
        ks = jax.random.split(key, 6)
        return {'x': jax.random.normal(ks[0], (B, S, IN), jnp.float32), 'W_org': jax.random.normal(ks[1], (OUT, IN), jnp.float32) * 0.02, 'lora_down': jax.random.normal(ks[2], (E, IN, R), jnp.float32) * 0.02, 'lora_up': jax.random.normal(ks[3], (E, R, OUT), jnp.float32) * 0.02, 'lora_keys': jax.random.normal(ks[4], (E, K), jnp.float32), 'Wq': jax.random.normal(ks[5], (K, IN), jnp.float32) * 0.02}
    _L0_ffn_in = _L0_ffn_setup()
    _d = {'L0_attn_hidden_states': _L0_attn_in['hidden_states'], 'L0_attn_wq': _L0_attn_in['wq'], 'L0_attn_wk': _L0_attn_in['wk'], 'L0_attn_wv': _L0_attn_in['wv'], 'L0_attn_wo': _L0_attn_in['wo'], 'L0_ffn_W_org': _L0_ffn_in['W_org'], 'L0_ffn_lora_down': _L0_ffn_in['lora_down'], 'L0_ffn_lora_up': _L0_ffn_in['lora_up'], 'L0_ffn_lora_keys': _L0_ffn_in['lora_keys'], 'L0_ffn_Wq': _L0_ffn_in['Wq']}
    _x0 = _d['L0_attn_hidden_states']
    _d['L0_attn_hidden_states'] = jax.random.normal(jax.random.fold_in(jax.random.key(seed), 1), (2, 1024, 512), dtype=_x0.dtype)
    del _x0
    return _d

def reference(L0_attn_hidden_states, L0_attn_wq, L0_attn_wk, L0_attn_wv, L0_attn_wo, L0_ffn_W_org, L0_ffn_lora_down, L0_ffn_lora_up, L0_ffn_lora_keys, L0_ffn_Wq):

    def _L0_attn_ref(hidden_states, wq, wk, wv, wo):
        import jax, jax.numpy as jnp
        import numpy as np
        N_HEADS = 32
        ROPE_THETA = 10000.0

        def _rope_cos_sin(sl, head_dim, dtype):
            inv_freq = 1.0 / ROPE_THETA ** (jnp.arange(0, head_dim, 2, dtype=jnp.float32) / head_dim)
            pos = jnp.arange(sl, dtype=jnp.float32)
            freqs = pos[:, None] * inv_freq[None, :]
            emb = jnp.concatenate([freqs, freqs], axis=-1)
            return (jnp.cos(emb).astype(dtype), jnp.sin(emb).astype(dtype))

        def _rotate_half(x):
            h = x.shape[-1] // 2
            return jnp.concatenate([-x[..., h:], x[..., :h]], axis=-1)
        bs, sl, hs = hidden_states.shape
        hd = hs // N_HEADS
        q = hidden_states @ wq
        k = hidden_states @ wk
        v = hidden_states @ wv
        q = q.reshape(bs, sl, N_HEADS, hd)
        k = k.reshape(bs, sl, N_HEADS, hd)
        v = v.reshape(bs, sl, N_HEADS, hd)
        cos, sin = _rope_cos_sin(sl, hd, hidden_states.dtype)
        cos = cos[None, :, None, :]
        sin = sin[None, :, None, :]
        q = q * cos + _rotate_half(q) * sin
        k = k * cos + _rotate_half(k) * sin
        q = q.transpose(0, 2, 1, 3)
        k = k.transpose(0, 2, 1, 3)
        v = v.transpose(0, 2, 1, 3)
        scores = jnp.einsum('bhqd,bhkd->bhqk', q, k) / jnp.sqrt(jnp.asarray(hd, q.dtype))
        causal = jnp.tril(jnp.ones((sl, sl), dtype=bool))
        scores = jnp.where(causal[None, None], scores, jnp.finfo(scores.dtype).min)
        attn = jax.nn.softmax(scores, axis=-1)
        out = jnp.einsum('bhqk,bhkd->bhqd', attn, v)
        out = out.transpose(0, 2, 1, 3).reshape(bs, sl, hs)
        return out @ wo

    def _L0_ffn_ref(x, W_org, lora_down, lora_up, lora_keys, Wq):
        import jax, jax.numpy as jnp
        import numpy as np
        import math
        B, S, IN, OUT = (4, 256, 512, 512)
        E, R, K = (8, 64, 128)
        SCALE = 64.0 / 64.0
        MULTIPLIER = 1.0
        base = jnp.einsum('bsi,oi->bso', x, W_org)
        q = jnp.einsum('bi,ki->bk', x.mean(axis=1), Wq)
        scores = jnp.einsum('bk,ek->be', q, lora_keys) / math.sqrt(K)
        coeffs = jax.nn.softmax(scores, axis=-1)
        h = jnp.einsum('bsi,eir->bser', x, lora_down)
        delta = jnp.einsum('be,bser,ero->bso', coeffs, h, lora_up)
        return base + delta * (SCALE * MULTIPLIER)
    x = L0_attn_hidden_states
    x = x + _L0_attn_ref(_layernorm(x, axis=-1), L0_attn_wq, L0_attn_wk, L0_attn_wv, L0_attn_wo)
    x = x + _L0_ffn_ref(_layernorm(x, axis=-1), L0_ffn_W_org, L0_ffn_lora_down, L0_ffn_lora_up, L0_ffn_lora_keys, L0_ffn_Wq)
    return x

_drawn_inputs = setup_inputs


def setup_inputs(seed=0):
    import zlib

    import numpy as np

    out = dict(_drawn_inputs(seed))
    spreads = {}
    factors = {'L0_ffn_lora_keys': 23.6, 'L0_ffn_Wq': 27.221}
    for name, (base, spread) in spreads.items():
        noise = np.random.default_rng([zlib.crc32(name.encode()), seed]).standard_normal(out[name].shape)
        drawn = base * np.exp(spread * noise) if base else spread * noise
        out[name] = jnp.asarray(drawn.astype(out[name].dtype))
    for name, factor in factors.items():
        out[name] = (out[name] * factor).astype(out[name].dtype)
    return out
```

```python
from contextlib import ExitStack

import concourse.bass as bass
from concourse import mybir

ALU = mybir.AluOpType
ACT = mybir.ActivationFunctionType
AX = mybir.AxisListType
F32 = mybir.dt.float32
F32R = mybir.dt.float32r
BF16 = mybir.dt.bfloat16

P = 128
HEADS = 32
THETA = 10000.0
EPS = 1e-5
EXPERTS, RANK, KEY = 8, 64, 128


def wait(eng, sem, value, apart=False):
    if isinstance(value, int):
        if value > 0:
            eng.wait_ge(sem, value)
        return
    eng.wait_ge(sem, value)
    if apart:
        eng.nop(nofuse=True)


class Sizes:

    def __init__(s, batches, seq, dim):
        s.B, s.S, s.D = batches, seq, dim
        s.HD = dim // HEADS
        s.HALF = s.HD // 2
        s.DC = dim // P
        s.CT = 512
        s.NC = seq // s.CT
        s.TT = s.CT // P
        s.CHUNKS = batches * s.NC
        s.SG = HEADS // 16
        s.GH = 4
        s.GB = HEADS // s.GH
        s.G = batches * s.GB
        s.KT = seq // P
        s.ROWS = 6 * s.HD


Q_RUNS = [(0, 3), (0, 2), (0, 1)]
K_PARTS = [(0, 3), (1, 2), (2, 1)]


def layer_kernel(nc, x, xc, w_in, rope, w_o, w_org_t, down_t, up, keys_t, wq_t, out):
    z = Sizes(*x.shape)
    scratch = {n: nc.dram_tensor(f"{n}_parts", [z.NC * z.G, 3, 2, z.HALF, z.GH, z.CT], BF16,
                                 kind="Internal").ap() for n in "qk"}
    with ExitStack() as keep:
        def sb(name, shape, dt):
            return keep.enter_context(nc.sbuf_tensor(name, shape, dt))

        def sem(name):
            return keep.enter_context(nc.semaphore(name))

        c = {
            "ident": sb("ident", [P, P], F32),
            "ident_b": sb("ident_b", [P, P], BF16),
            "causal": sb("causal", [P, P], BF16),
            "wo": sb("wo", [P, z.DC, z.D], F32),
            "w_org": sb("w_org", [P, z.DC, z.D], F32),
            "down": sb("down", [P, z.DC, z.D], F32),
            "up": sb("up", [P, z.DC, z.D], F32),
            "wq": sb("wq_gate", [P, z.DC, KEY], F32),
            "keys": sb("keys", [KEY, EXPERTS], F32),
            "s_weights": sem("weights_loaded"),
            "s_const": sem("constants_ready"),
        }
        values = sb("values", [P, z.NC, z.G, z.TT, z.GH * z.HD], F32)
        project_phase(nc, z, c, xc, w_in, rope, (w_o, w_org_t, down_t, up, keys_t, wq_t), scratch, values)
        attn_t = sb("attn_t", [P, z.B * z.DC, z.S], F32)
        attention_phase(nc, z, c, scratch, values, attn_t)
        ffn_phase(nc, z, c, x, values, attn_t, out)



def project_phase(nc, z, c, xc, w_in, rope, weights, scratch, values):
    NU = 2 * z.SG
    QKC = 2 * z.D
    with ExitStack() as ctx:
        def sb(name, shape, dt):
            return ctx.enter_context(nc.sbuf_tensor(name, shape, dt))

        def sem(name):
            return ctx.enter_context(nc.semaphore(name))

        wraw = sb("wraw", [P, 3 * z.D], F32)
        whi = sb("whi", [P, z.DC, 3 * z.D], F32R)
        wlo = sb("wlo", [P, z.DC, 3 * z.D], F32R)
        xin = sb("xin", [P, z.TT, z.D], F32)
        xn = sb("xn", [P, z.TT, z.D], F32)
        xhi = sb("xhi", [P, z.DC, z.CT], F32R)
        xlo = sb("xlo", [P, z.DC, z.CT], F32R)
        table = sb("table", [P, 2, z.CT], F32)
        prod = sb("prod", [P, 2, 4, z.CT], F32)
        rot = sb("rot", [P, 2, 2, z.CT], F32)
        rest = sb("rest", [P, 2, z.CT], F32)
        parts = sb("parts", [P, 2, 3, 2, z.CT], BF16)
        stats = sb("stats", [P, z.TT, 6], F32)
        mv = sb("mv", [P, z.TT, 2], F32)
        small = sb("small", [P, 4, z.TT], F32)

        pt = ctx.enter_context(nc.psum_tensor("pt", [P, 2, z.DC, P], F32))
        pu = ctx.enter_context(nc.psum_tensor("pu", [P, 2, 2, z.CT], F32))
        pv = ctx.enter_context(nc.psum_tensor("pv", [P, 2, z.D], F32))

        s_wraw = sem("wraw_loaded")
        s_whi = sem("whi_ready")
        s_wlo = sem("wlo_ready")
        s_x = sem("x_loaded")
        s_table = sem("table_loaded")
        s_ln = sem("ln_small")
        s_sqrt = sem("sqrt_ready")
        s_xn = sem("xn_ready")
        s_tr = sem("transposed")
        s_xhi = sem("xhi_ready")
        s_xlo = sem("xlo_ready")
        s_unit = sem("unit_projected")
        s_v = sem("v_projected")
        s_vout = sem("v_stored")
        s_prod = sem("products_ready")
        s_rot = sem("rotated")
        s_p1 = sem("part1_ready")
        s_rest = sem("rest_ready")
        s_p2 = sem("part2_ready")
        s_p3 = sem("part3_ready")
        s_put = [sem("parts_stored_even"), sem("parts_stored_odd")]
        s_setup = sem("pool_setup")

        LN_STEPS = 6 + 2
        block = ctx.enter_context(nc.Block())

        @block.sync
        def _(sp):
            def load_x(i):
                wait(sp, s_xn, z.TT * i)
                sp.dma_start(xin[:, :, :], xc[bass.ds(i, 1)].rearrange("a (t p) d -> p (a t) d", p=P)).then_inc(s_x, 16)

            def load_table(i):
                wait(sp, s_prod, NU * 2 * i)
                sp.dma_start(table[:, :, :], rope[bass.ds(i, 1)].rearrange("a p s t -> p (a s) t")).then_inc(s_table, 16)

            def store_parts(i):
                for u in range(NU):
                    to = scratch["qk"[u // z.SG]]
                    g = u % z.SG
                    wait(sp, s_p3, NU * i + u + 1)
                    for part in range(3):
                        for half in range(2):
                            dst = to[bass.ds(i * z.GB + g * z.GH, z.GH), part, half].rearrange("g e h t -> g (e h) t")
                            sp.dma_start(dst, parts[:, u % 2, part, half, :]).then_inc(s_put[u % 2], 16)

            load_x(0)
            for kc in range(z.DC):
                wait(sp, s_wlo, kc)
                sp.dma_start(wraw[:, :], w_in[kc * P:(kc + 1) * P, :]).then_inc(s_wraw, 16)
            load_table(0)
            w_o, w_org_t, down_t, up, keys_t, wq_t = weights
            with sp.Fori(0, z.CHUNKS - 1) as i:
                load_x(i + 1)
                store_parts(i)
                load_table(i + 1)
            for name, src in (("wo", w_o), ("w_org", w_org_t), ("down", down_t), ("up", up), ("wq", wq_t)):
                sp.dma_start(c[name][:, :, :], src.rearrange("(a p) n -> p a n", p=P)).then_inc(c["s_weights"], 16)
            sp.dma_start(c["keys"][:, :], keys_t).then_inc(c["s_weights"], 16)
            store_parts(z.CHUNKS - 1)
            for par in range(2):
                sp.wait_ge(s_put[par], z.CHUNKS * NU // 2 * 6 * 16)
            sp.wait_ge(c["s_weights"], 6 * 16)

        @block.gpsimd
        def _(pool):
            pool.memset(c["ident"][:, :], 0.0).then_inc(s_setup, 1)
            pool.memset(c["ident_b"][:, :], 0.0).then_inc(s_setup, 1)
            pool.memset(c["causal"][:, :], 0.0).then_inc(s_setup, 1)
            pool.wait_ge(s_setup, 3)
            for m in (c["ident"], c["ident_b"]):
                pool.affine_select(out=m[:, :], in_=m[:, :], compare_op=ALU.not_equal, fill=1.0, base=0,
                                   pattern=[[-1, P]], channel_multiplier=1).then_inc(c["s_const"], 1)
            pool.affine_select(out=c["causal"][:, :], in_=c["causal"][:, :], compare_op=ALU.is_ge, fill=-3e38,
                               base=0, pattern=[[-1, P]], channel_multiplier=1).then_inc(c["s_const"], 1)

            def rotate(i):
                for u in range(NU):
                    n = NU * i + u
                    pr, ro = prod[:, u % 2], rot[:, u % 2]
                    wait(pool, s_rest, n - 1)
                    wait(pool, s_prod, 2 * n + 1)
                    pool.tensor_tensor(ro[:, 0], pr[:, 0], pr[:, 1], ALU.subtract).then_inc(s_rot, 1)
                    wait(pool, s_prod, 2 * n + 2)
                    pool.tensor_tensor(ro[:, 1], pr[:, 2], pr[:, 3], ALU.add).then_inc(s_rot, 1)

            rotate(0)
            with pool.Fori(1, z.CHUNKS) as i:
                rotate(i)

        @block.scalar
        def _(act):
            def root(i):
                wait(act, s_ln, LN_STEPS * i + 3)
                act.activation(small[:, 1], small[:, 0], ACT.Sqrt).then_inc(s_sqrt, 1)

            def upper(i):
                wait(act, s_v, z.TT * i)
                for t in range(z.TT):
                    wait(act, s_tr, z.TT * i + t + 1)
                    act.copy(xhi[:, :, t * P:(t + 1) * P], pt[:, t % 2]).then_inc(s_xhi, 1)

            def parts12(i, u):
                n = NU * i + u
                wait(act, s_put[u % 2], (i * (NU // 2) + u // 2) * 96)
                wait(act, s_rot, 2 * n + 2)
                act.copy(parts[:, u % 2, 0], rot[:, u % 2]).then_inc(s_p1, 1)
                wait(act, s_rest, n + 1)
                act.copy(parts[:, u % 2, 1], rest[:, :, :]).then_inc(s_p2, 1)

            def store_v(i):
                for t in range(z.TT):
                    wait(act, s_v, z.TT * i + t + 1)
                    act.copy(values[:, :, :, :, :].rearrange("p n g t f -> p (n g) t f")[:, bass.ds(i * z.GB, z.GB), t, :],
                             pv[:, t % 2].rearrange("p (g f) -> p g f", g=z.GB)).then_inc(s_vout, 1)

            act.wait_ge(s_wraw, 16)
            for kc in range(z.DC):
                wait(act, s_wraw, 16 * (kc + 1))
                act.copy(whi[:, kc], wraw[:, :]).then_inc(s_whi, 1)
                if kc == 0:
                    root(0)
            upper(0)

            def body(i):
                for u in range(NU):
                    parts12(i, u)
                    if u == 2:
                        root(i + 1)
                store_v(i)
                upper(i + 1)

            body(0)
            with act.Fori(1, z.CHUNKS - 1) as i:
                body(i)
            for u in range(NU):
                parts12(z.CHUNKS - 1, u)
            store_v(z.CHUNKS - 1)

        @block.vector
        def _(dve):
            def ln_stats(i):
                base = LN_STEPS * i
                wait(dve, s_x, 16 * (i + 1), apart=True)
                for t in range(z.TT):
                    ins = dve.bn_stats(stats[:, t, :], xin[:, t, :])
                ins.then_inc(s_ln, 1)
                wait(dve, s_ln, base + 1, apart=True)
                for t in range(z.TT):
                    ins = dve.bn_aggr(mv[:, t, :], stats[:, t, :])
                ins.then_inc(s_ln, 1)
                wait(dve, s_ln, base + 2)
                dve.tensor_scalar(small[:, 0], mv[:, :, 1], EPS, None, ALU.add).then_inc(s_ln, 1)

            def ln_apply(i):
                rsqrt_newton(dve, [small[:, n] for n in range(4)], s_ln, LN_STEPS * i + 3, s_sqrt, i + 1)
                wait(dve, s_tr, z.TT * i)
                for t in range(z.TT):
                    dve.tensor_scalar(xn[:, t, :], xin[:, t, :], mv[:, t, 0:1], small[:, 3, t:t + 1],
                                      ALU.subtract, ALU.mult).then_inc(s_xn, 1)

            def lower(i):
                for t in range(z.TT):
                    wait(dve, s_xhi, z.TT * i + t + 1)
                    hi = xhi[:, :, t * P:(t + 1) * P]
                    dve.tensor_tensor(xlo[:, :, t * P:(t + 1) * P], pt[:, t % 2], hi.bitcast(F32),
                                      ALU.subtract).then_inc(s_xlo, 1)

            def products(i, u, half):
                n = NU * i + u
                a, b = pu[:, u % 2, 0, :], pu[:, u % 2, 1, :]
                if half == 0:
                    wait(dve, s_unit, n + 1)
                    wait(dve, s_rot, 2 * n - 2)
                    dve.tensor_tensor(prod[:, u % 2, 0], a, table[:, 0], ALU.mult)
                    dve.tensor_tensor(prod[:, u % 2, 1], b, table[:, 1], ALU.mult).then_inc(s_prod, 1)
                else:
                    dve.tensor_tensor(prod[:, u % 2, 2], b, table[:, 0], ALU.mult)
                    dve.tensor_tensor(prod[:, u % 2, 3], a, table[:, 1], ALU.mult).then_inc(s_prod, 1)

            def rest_of(i, u):
                n = NU * i + u
                wait(dve, s_p3, n)
                wait(dve, s_p1, n + 1)
                dve.tensor_tensor(rest[:, :, :], rot[:, u % 2], parts[:, u % 2, 0], ALU.subtract).then_inc(s_rest, 1)

            def part3(i, u):
                n = NU * i + u
                wait(dve, s_p2, n + 1)
                dve.tensor_tensor(parts[:, u % 2, 2], rest[:, :, :], parts[:, u % 2, 1], ALU.subtract).then_inc(s_p3, 1)

            def units(i, more):
                wait(dve, s_table, 16 * (i + 1))
                for u in range(NU):
                    products(i, u, 0)
                    if u:
                        rest_of(i, u - 1)
                    products(i, u, 1)
                    if u:
                        part3(i, u - 1)
                    if u == 1 and more:
                        ln_stats(i + 1)
                rest_of(i, NU - 1)
                if more:
                    ln_apply(i + 1)
                part3(i, NU - 1)

            ln_stats(0)
            ln_apply(0)
            for kc in range(z.DC):
                wait(dve, s_whi, kc + 1)
                dve.tensor_tensor(wlo[:, kc], wraw[:, :], whi[:, kc].bitcast(F32), ALU.subtract).then_inc(s_wlo, 1)
            lower(0)
            units(0, True)
            with dve.Fori(1, z.CHUNKS - 1) as i:
                wait(dve, s_v, z.TT * i)
                lower(i)
                units(i, True)
            wait(dve, s_v, z.TT * (z.CHUNKS - 1))
            lower(z.CHUNKS - 1)
            units(z.CHUNKS - 1, False)

        @block.tensor
        def _(pe):
            pe.wait_ge(c["s_const"], 3)

            def transposes(i):
                for t in range(z.TT):
                    wait(pe, s_xn, z.TT * i + t + 1)
                    wait(pe, s_xlo, z.TT * i + t - 1)
                    for k in range(z.DC):
                        mm = pe.transpose(pt[:, t % 2, k, :], xn[:, t, k * P:(k + 1) * P], c["ident"][:, :])
                    mm.then_inc(s_tr, 1)

            def project(i):
                wait(pe, s_xlo, z.TT * (i + 1))
                for u in range(NU):
                    n = NU * i + u
                    wait(pe, s_prod, 2 * n - 2)
                    for half in range(2):
                        col = slice(u * 256 + half * P, u * 256 + (half + 1) * P)
                        for k in range(z.DC):
                            if half == 0 and u == 0 and isinstance(i, int) and i == 0:
                                wait(pe, s_wlo, k + 1)
                            mm = exact_product(pe, pu[:, u % 2, half, :], whi[:, k, col], wlo[:, k, col],
                                               xhi[:, k, :], xlo[:, k, :], k == 0, k == z.DC - 1)
                    mm.then_inc(s_unit, 1)
                for t in range(z.TT):
                    wait(pe, s_vout, z.TT * i + t - 1)
                    tok = slice(t * P, (t + 1) * P)
                    for k in range(z.DC):
                        mm = exact_product(pe, pv[:, t % 2, :], xhi[:, k, tok], xlo[:, k, tok],
                                           whi[:, k, QKC:], wlo[:, k, QKC:], k == 0, k == z.DC - 1)
                    mm.then_inc(s_v, 1)

            transposes(0)
            project(0)
            transposes(1)
            with pe.Fori(1, z.CHUNKS - 1) as i:
                project(i)
                transposes(i + 1)
            project(z.CHUNKS - 1)


def exact_product(pe, out, a_hi, a_lo, b_hi, b_lo, first, last):
    pe.matmul(out, a_hi, b_hi, start=first, stop=False)
    pe.matmul(out, a_hi, b_lo, start=False, stop=False)
    return pe.matmul(out, a_lo, b_hi, start=False, stop=last)


def rsqrt_newton(dve, small, s_step, base, s_sqrt, roots):
    v, s0, t, r = small
    wait(dve, s_sqrt, roots)
    dve.reciprocal(t, s0).then_inc(s_step, 1)
    wait(dve, s_step, base + 1)
    dve.tensor_tensor(t, t, v, ALU.mult).then_inc(s_step, 1)
    wait(dve, s_step, base + 2)
    dve.tensor_tensor(t, t, s0, ALU.add).then_inc(s_step, 1)
    wait(dve, s_step, base + 3)
    dve.reciprocal(r, t).then_inc(s_step, 1)
    wait(dve, s_step, base + 4)
    dve.tensor_scalar(r, r, 2.0, None, ALU.mult).then_inc(s_step, 1)
    wait(dve, s_step, base + 5)



def attention_phase(nc, z, c, scratch, values, attn_t):
    STEPS = [(qc, kb) for qc in range(z.NC) for kb in range(z.TT * (qc + 1))]
    NS = len(STEPS)
    RING = 3
    LAG = 2
    QT, HG = z.TT, z.GH
    MROWS = 3 * HG * QT

    tiles = []
    for qc in range(z.NC):
        for qt in range(QT):
            for kc in range(qc + 1):
                width = z.CT if kc < qc else (qt + 1) * P
                n = z.CT // width
                tiles.append([(qc, qt, kc, width, h, min(n, HG - h)) for h in range(0, HG, n)])
    chunk_tiles = [sum(tiles[:QT], []), sum(tiles[QT:], [])]
    AFTER = 4
    LATE = 4
    ahead = chunk_tiles[0] + chunk_tiles[1][:AFTER] + ["turn 0"] + chunk_tiles[1][AFTER:-LATE]
    late = chunk_tiles[1][-LATE:] + ["turn 1"]
    NA, NI = len(ahead), len(ahead) + len(late)
    T0 = len(chunk_tiles[0])
    assert NI % 2 == 0
    LATE_IN = {0: (0, LATE), 2: (LATE, LATE + 1)}
    cuts = [0, 5, 10, 15, 20, 25, 29, 32, NA]
    AHEAD_IN = {4 + n: (cuts[n], cuts[n + 1]) for n in range(8)}
    MASKED = [s for s, (qc, kb) in enumerate(STEPS) if kb >= z.TT * qc]

    def q0(step):
        qc, kb = STEPS[step]
        return max(0, kb - z.TT * qc) * P

    with ExitStack() as ctx:
        def sb(name, shape, dt):
            return ctx.enter_context(nc.sbuf_tensor(name, shape, dt))

        def sem(name):
            return ctx.enter_context(nc.semaphore(name))

        qs = [sb(f"q_stack{n}", [P, z.NC, HG, z.CT], BF16) for n in range(2)]
        ks = [sb(f"k_stack{n}", [P, z.NC, HG, z.CT], BF16) for n in range(2)]
        probs = [sb(f"probs{n}", [P, HG, z.CT], F32) for n in range(RING)]
        vg = [sb(f"v_group{n}", [P, z.KT, HG, 2 * z.HD], F32) for n in range(2)]
        raw = [sb(f"out_raw{n}", [P, z.CT], F32) for n in range(z.NC)]
        num = sb("numerator", [P, z.S], F32)
        den = sb("denominator", [P, z.S], F32)
        top = sb("row_max", [P, 2, z.NC, HG, QT], F32)
        top2 = sb("row_max_late", [P, 2, HG, QT], F32)
        neg = sb("neg_parts", [P, z.NC, 3, HG, QT], BF16)
        left = sb("neg_left", [P, z.NC, 2, HG * QT], F32)
        rows = [sb(f"neg_rows{n}", [MROWS, P], BF16) for n in range(z.NC)]

        st = [ctx.enter_context(nc.psum_tensor(f"scores_t{n}", [P, 2, z.CT], F32)) for n in range(2)]
        po = [ctx.enter_context(nc.psum_tensor(f"out_t{n}", [P, z.CT], F32)) for n in range(z.NC)]
        pm = [ctx.enter_context(nc.psum_tensor(f"max_bank{n}", [P, z.CT], F32)) for n in range(2)]

        s_ones = sem("ones_ready")
        s_stack = [sem(f"stack_loaded{n}") for n in range(2)]
        s_item = sem("max_bank_filled")
        s_taken = sem("max_bank_read")
        s_comb = sem("max_combined")
        s_neg = sem("neg_steps")
        s_rows = [sem(f"neg_rows_loaded{n}") for n in range(z.NC)]
        s_qk = sem("scores_ready")
        s_exp = sem("exp_done")
        s_mask = sem("masked")
        s_pv = sem("pv_done")
        s_vg = sem("v_group_ready")
        s_raw = [sem(f"out_raw_ready{n}") for n in range(z.NC)]
        s_dense = [sem(f"dense_loaded{n}") for n in range(z.NC)]
        s_inv = sem("reciprocal_ready")
        s_norm = sem("normalized")

        NEG_STEPS = 5
        ITERS = z.G // 2
        DENSE = 2 * HG * 16

        block = ctx.enter_context(nc.Block())

        def run(eng, body):
            body(0, True, False)
            with eng.Fori(1, ITERS - 1) as it:
                body(it, False, False)
            body(ITERS - 1, False, True)

        @block.sync
        def _(sp):
            def load_stacks(g, par):
                wait(sp, s_qk, 2 * NS * (g - 1))
                own_q, own_k = (scratch[n].rearrange("(c g) s f e h t -> g (s f e) c (h t)", c=z.NC)
                                [bass.ds(g, 1)].rearrange("a r c t -> (a r) c t") for n in "qk")
                row = 0
                for part, n in Q_RUNS:
                    sp.dma_start(qs[par][row:row + z.HD * n].rearrange("p c h t -> p c (h t)"),
                                 own_q[z.HD * part:z.HD * (part + n)]).then_inc(s_stack[par], 16)
                    row += z.HD * n
                row = 0
                for part, times in K_PARTS:
                    for _ in range(times):
                        sp.dma_start(ks[par][row:row + z.HD].rearrange("p c h t -> p c (h t)"),
                                     own_k[z.HD * part:z.HD * (part + 1)]).then_inc(s_stack[par], 16)
                        row += z.HD

            def body(it, first, last):
                for par in range(2):
                    g = 2 * it + par
                    if not (first and par == 0):
                        if not (last and par == 1):
                            load_stacks(g + 1, 1 - par)
                        dense_at(it, par, g, 1, True)
                    dense_at(it, par, g, 0, False)

            def dense_at(it, par, g, qc, before):
                gg = g - 1 if before else g
                pp = 1 - par if before else par
                wait(sp, s_raw[qc], gg + 1)
                if pp == 0:
                    wait(sp, s_norm, it)
                for h in range(HG):
                    to = slice(64 * pp + 16 * h, 64 * pp + 16 * h + 16)
                    for buf, off in ((num, 0), (den, 16)):
                        sp.dma_start(buf[to, qc * z.CT:(qc + 1) * z.CT],
                                     raw[qc][32 * h + off:32 * h + off + 16, :]).then_inc(s_dense[qc], 16)

            load_stacks(0, 0)
            load_stacks(1, 1)
            run(sp, body)
            dense_at(ITERS, 0, z.G, 1, True)
            for qc in range(z.NC):
                sp.wait_ge(s_dense[qc], z.G * DENSE)

        @block.gpsimd
        def _(pool):
            pool.memset(vg[0][:, :, :, z.HD:], 1.0).then_inc(s_ones, 1)
            pool.memset(vg[1][:, :, :, z.HD:], 1.0).then_inc(s_ones, 1)
            pool.wait_ge(s_ones, 2)
            pool.memset(ks[0][z.ROWS:, :, :, :], 1.0).then_inc(s_ones, 1)
            pool.memset(ks[1][z.ROWS:, :, :, :], 1.0).then_inc(s_ones, 1)
            pool.wait_ge(s_ones, 4)

            def copy_v(g, par):
                wait(pool, s_pv, NS * (g - 1))
                v = values[:, :, :, :, :].rearrange("p c g t f -> p g c (t f)")[:, bass.ds(g, 1)]
                pool.tensor_copy(vg[par][:, :, :, 0:z.HD].rearrange("p (c t) h f -> p c (t h) f", c=z.NC),
                                 v.rearrange("p a c (n f) -> p (a c) n f", f=z.HD)).then_inc(s_vg, 1)

            def negate(g, par, qc):
                base = NEG_STEPS * (z.NC * g + qc)
                if qc == 0:
                    wait(pool, s_taken, NI * g + T0, apart=True)
                else:
                    wait(pool, s_comb, g + 1, apart=True)
                m = top[:, par, qc].rearrange("p h t -> p (h t)")
                part = [neg[:, qc, n].rearrange("p h t -> p (h t)") for n in range(3)]
                rest = [left[:, qc, n] for n in range(2)]
                wait(pool, s_taken, NI * (g - 1) + (T0 + AFTER + 1 if qc == 0 else NI), apart=True)
                src = m
                for n in range(3):
                    pool.tensor_scalar(part[n], src, -1.0, 1.0, ALU.mult, ALU.mult).then_inc(s_neg, 1)
                    if n < 2:
                        wait(pool, s_neg, base + 2 * n + 1)
                        pool.tensor_tensor(rest[n], src, part[n], ALU.add).then_inc(s_neg, 1)
                        wait(pool, s_neg, base + 2 * n + 2, apart=True)
                        src = rest[n]

            def mask(g, step):
                wait(pool, s_exp, 2 * (NS * g + step) + 2, apart=True)
                t = probs[step % RING][:, :, 0:P]
                pool.affine_select(out=t, in_=t, compare_op=ALU.is_ge, fill=0.0, base=0,
                                   pattern=[[0, HG], [1, P]], channel_multiplier=-1).then_inc(s_mask, 1)

            def normalize(it):
                wait(pool, s_inv, it + 1)
                pool.tensor_tensor(attn_t[:, bass.ds(it, 1), :].rearrange("p a t -> p (a t)"),
                                   num[:, :], den[:, :], ALU.mult).then_inc(s_norm, 1)

            def body(it, first, last):
                for par in range(2):
                    g = 2 * it + par
                    for step in range(NS):
                        if step in MASKED:
                            mask(g, step)
                        if step == 1:
                            negate(g, par, 1)
                        if step == 3 and not (last and par == 1):
                            copy_v(g + 1, 1 - par)
                        if step == 6 and not (last and par == 1):
                            negate(g + 1, 1 - par, 0)
                        if step == 7 and par == 0 and not first:
                            normalize(it - 1)

            copy_v(0, 0)
            negate(0, 0, 0)
            run(pool, body)
            normalize(ITERS - 1)

        @block.scalar
        def _(act):
            def exps(g, step):
                n = NS * g + step
                w = z.CT - q0(step)
                wait(act, s_pv, n - RING + 1)
                for pair in range(2):
                    wait(act, s_qk, 2 * n + pair + 1)
                    act.activation(probs[step % RING][:, 2 * pair:2 * pair + 2, 0:w], st[pair][:, :, 0:w],
                                   ACT.Exp, scale=z.HD ** -0.5).then_inc(s_exp, 1)

            def evacuate(g, qc):
                wait(act, s_pv, NS * g + (z.TT if qc == 0 else NS))
                wait(act, s_dense[qc], DENSE * g)
                act.copy(raw[qc][:, :], po[qc][:, :]).then_inc(s_raw[qc], 1)

            def load_rows(g, par, qc):
                wait(act, s_taken, NI * g + (T0 + AFTER + 1 if qc == 0 else NI))
                act.dma_start(qs[par][z.ROWS:z.ROWS + 3, qc], rows[qc][:, :]).then_inc(s_rows[qc], 16)

            def body(it, first, last):
                for par in range(2):
                    g = 2 * it + par
                    for step in range(NS):
                        exps(g, step)
                        if step == LAG and not (first and par == 0):
                            evacuate(g - 1, 1)
                        if step == 3:
                            load_rows(g, par, 1)
                        if step == z.TT + LAG:
                            evacuate(g, 0)
                        if step == 9 and not (last and par == 1):
                            load_rows(g + 1, 1 - par, 0)

            load_rows(0, 0, 0)
            run(act, body)
            evacuate(z.G - 1, 1)

        @block.vector
        def _(dve):
            def take(g, par, items, first):
                for n, item in enumerate(items):
                    k = NI * g + first + n
                    bank = pm[(first + n) % 2]
                    wait(dve, s_item, k + 1)
                    if item == "turn 0" or item == "turn 1":
                        qc = int(item[-1])
                        wait(dve, s_rows[qc], 16 * g)
                        dve.tensor_copy(rows[qc][:, :], bank[0:MROWS, 0:P // 2].bitcast(BF16)).then_inc(s_taken, 1)
                        continue
                    qc, qt, kc, width, h, n_heads = item
                    to = (top2[:, par] if kc < qc else top[:, par, qc])[:, h:h + n_heads, qt]
                    dve.reduce_max(to, bank[:, 0:n_heads * width].rearrange("p (h k) -> p h k", h=n_heads),
                                   AX.X).then_inc(s_taken, 1)
                    if first + n == NI - 2:
                        wait(dve, s_taken, k + 1)
                        m = top[:, par, 1].rearrange("p h t -> p (h t)")
                        dve.tensor_tensor(m, m, top2[:, par].rearrange("p h t -> p (h t)"), ALU.max).then_inc(s_comb, 1)

            def invert(it):
                for qc in range(z.NC):
                    wait(dve, s_dense[qc], DENSE * 2 * (it + 1))
                dve.reciprocal(den[:, :], den[:, :]).then_inc(s_inv, 1)

            def body(it, first, last):
                for par in range(2):
                    g = 2 * it + par
                    for step in range(NS):
                        if step in LATE_IN:
                            a, b = LATE_IN[step]
                            take(g, par, late[a:b], NA + a)
                        if step == 7 and par == 0 and not first:
                            invert(it - 1)
                        if step in AHEAD_IN and not (last and par == 1):
                            a, b = AHEAD_IN[step]
                            take(g + 1, 1 - par, ahead[a:b], a)

            take(0, 0, ahead, 0)
            run(dve, body)
            invert(ITERS - 1)

        @block.tensor
        def _(pe):
            def fill(g, par, items, first):
                for n, item in enumerate(items):
                    k = NI * g + first + n
                    bank = pm[(first + n) % 2]
                    wait(pe, s_taken, k - 1)
                    if item == "turn 0" or item == "turn 1":
                        qc = int(item[-1])
                        wait(pe, s_neg, NEG_STEPS * (z.NC * g + qc + 1), apart=True)
                        pe.transpose(bank[0:MROWS, 0:P // 2].bitcast(BF16),
                                     neg[:, qc].rearrange("p s h t -> p (s h t)"), c["ident_b"][:, :]).then_inc(s_item, 1)
                        continue
                    qc, qt, kc, width, h0, n_heads = item
                    for j in range(n_heads):
                        to = bank[:, j * width:(j + 1) * width]
                        diagonal = kc == qc
                        mm = pe.matmul(to, qs[par][0:z.ROWS, qc, h0 + j, qt * P:(qt + 1) * P],
                                       ks[par][0:z.ROWS, kc, h0 + j, 0:width],
                                       start=(j == 0), stop=not diagonal, skip_group_check=True)
                        if diagonal:
                            mm = pe.matmul(to[:, width - P:], c["ident_b"][:, :], c["causal"][:, :],
                                           start=False, stop=True, skip_group_check=True)
                    mm.then_inc(s_item, 1)

            def scores(g, par, step):
                n = NS * g + step
                qc, kb = STEPS[step]
                if kb == 0:
                    wait(pe, s_rows[qc], 16 * (g + 1))
                for pair in range(2):
                    wait(pe, s_exp, 2 * n + pair - 1)
                    for h in (2 * pair, 2 * pair + 1):
                        mm = pe.matmul(st[pair][:, h % 2, 0:z.CT - q0(step)],
                                       ks[par][0:z.ROWS + 3, kb // z.TT, h, kb % z.TT * P:(kb % z.TT + 1) * P],
                                       qs[par][0:z.ROWS + 3, qc, h, q0(step):], start=True, stop=True)
                    mm.then_inc(s_qk, 1)

            def weigh(g, par, step):
                n = NS * g + step
                qc, kb = STEPS[step]
                wait(pe, s_exp, 2 * n + 2)
                if step in MASKED:
                    wait(pe, s_mask, len(MASKED) * g + MASKED.index(step) + 1)
                if kb == 0:
                    wait(pe, s_raw[qc], g)
                    if qc == 0:
                        wait(pe, s_vg, g + 1)
                for h in range(HG):
                    mm = pe.matmul(po[qc][32 * h:32 * h + 32, q0(step):], vg[par][:, kb, h, :],
                                   probs[step % RING][:, h, 0:z.CT - q0(step)],
                                   start=(kb == 0), stop=(kb == z.TT * (qc + 1) - 1))
                mm.then_inc(s_pv, 1)

            def body(it, first, last):
                for par in range(2):
                    g = 2 * it + par
                    for step in range(NS):
                        scores(g, par, step)
                        if step in LATE_IN:
                            a, b = LATE_IN[step]
                            fill(g, par, late[a:b], NA + a)
                        if step == z.TT and not (last and par == 1):
                            wait(pe, s_stack[1 - par], stack_count(it, par + 1))
                        if step in AHEAD_IN and not (last and par == 1):
                            a, b = AHEAD_IN[step]
                            fill(g + 1, 1 - par, ahead[a:b], a)
                        if step >= LAG:
                            weigh(g, par, step - LAG)
                        elif not (first and par == 0):
                            weigh(g - 1, 1 - par, NS - LAG + step)

            def stack_count(it, ahead_by):
                return 16 * (len(Q_RUNS) + z.ROWS // 16) * (it + ahead_by // 2 + 1)

            pe.wait_ge(s_ones, 4)
            pe.wait_ge(s_stack[0], stack_count(0, 0))
            fill(0, 0, ahead, 0)
            run(pe, body)
            for step in range(NS - LAG, NS):
                weigh(z.G - 1, 1, step)



def ffn_phase(nc, z, c, x, residual, attn_t, out):
    TILES = z.S // P
    ER = EXPERTS * RANK // P
    NT = z.B * TILES
    with ExitStack() as ctx:
        def sb(name, shape, dt):
            return ctx.enter_context(nc.sbuf_tensor(name, shape, dt))

        def sem(name):
            return ctx.enter_context(nc.semaphore(name))

        def pair(name, shape):
            return sb(name + "_hi", shape, F32R), sb(name + "_lo", shape, F32R)

        res = residual[:, :, :, :, :].rearrange("p c g t f -> p (c g t f)").rearrange("p (n d) -> p n d", n=NT)
        xt = sb("x2_t", [P, z.B * z.DC, z.S], F32)
        wo_hi, wo_lo = pair("w_o", [P, z.DC, z.D])
        dn_hi, dn_lo = pair("down_t", [P, ER, z.D])
        up_hi, up_lo = pair("up_scaled", [P, ER, z.D])
        wf_hi, wf_lo = pair("w_ffn", [P, z.DC, z.D])
        a_hi, a_lo = pair("tile", [P, 2, z.DC, P])
        xn, ot = c["wo"][:, 0:2, :], c["wo"][:, 2:4, :]
        wsum = c["down"]
        stats = sb("stats2", [P, 2, 6], F32)
        mv = sb("mv2", [P, 2, 2], F32)
        small = sb("small2", [P, 2, 4], F32)
        mean = sb("mean", [P, z.B * z.DC], F32)
        gate_q = sb("gate_q", [KEY, z.B], F32)
        soft = sb("soft", [z.B, 4, EXPERTS], F32)
        spread = sb("spread", [z.B, z.B, EXPERTS], F32)
        ones = sb("ones", [z.B, P], F32)
        coeff = sb("coeff", [P, z.B, ER], F32)

        py = ctx.enter_context(nc.psum_tensor("py", [P, 2, z.D], F32))
        pt = ctx.enter_context(nc.psum_tensor("pt2", [P, 2, z.DC, P], F32))
        pw = ctx.enter_context(nc.psum_tensor("pw", [P, 2, z.D], F32))
        pg = ctx.enter_context(nc.psum_tensor("pg", [P, 2, z.D], F32))

        s_x = [sem(f"x_back{b}") for b in range(z.B)]
        s_hi = sem("w_hi_ready")
        s_lo = sem("w_lo_ready")
        s_dlo = sem("down_lo_ready")
        s_ahi = sem("tile_hi_ready")
        s_alo = sem("tile_lo_ready")
        s_y = sem("y_ready")
        s_res = sem("residual_ready")
        s_ln = sem("ln2_stats")
        s_root = sem("ln2_root")
        s_sqrt = sem("sqrt2_ready")
        s_xn = sem("xn2_ready")
        s_tr = sem("transposed2")
        s_xt = sem("xt_ready")
        s_mean = sem("mean_ready")
        s_gate = sem("gate_pe")
        s_gv = sem("gate_vector")
        s_ge = sem("gate_exp")
        s_uhi = sem("up_hi_ready")
        s_ulo = sem("up_lo_ready")
        s_eff = sem("w_ffn_summed_pe")
        s_sum = sem("w_ffn_with_base")
        s_whi = sem("w_ffn_hi_ready")
        s_wlo = sem("w_ffn_lo_ready")
        s_zp = sem("ffn_product_ready")
        s_o = sem("out_tile_ready")
        s_out = [sem(f"out_stored{n}") for n in range(2)]

        LN_STEPS, ROOT_STEPS = 3, 5
        block = ctx.enter_context(nc.Block())

        def pairs(eng, b, body, between=None):
            body(b, 0)
            if between:
                between()
            with eng.Fori(1, TILES // 2) as m:
                body(b, m)

        def attn_tile(b, t):
            return attn_t[:, b * z.DC:(b + 1) * z.DC, bass.ds(t * P, P)]

        def xt_tile(b, t):
            return xt[:, b * z.DC:(b + 1) * z.DC, bass.ds(t * P, P)]

        @block.sync
        def _(sp):
            for b in range(z.B):
                sp.dma_start(res[:, b * TILES:(b + 1) * TILES, :],
                             x[b].rearrange("(t p) d -> p t d", p=P)).then_inc(s_x[b], 16)
            dst = out.rearrange("b (t p) d -> (b t) p d", p=P)
            with sp.Fori(0, NT // 2) as n:
                for j in range(2):
                    sp.wait_ge(s_o, 2 * n + j + 1)
                    sp.dma_start(dst[bass.ds(2 * n + j, 1)].rearrange("a p d -> (a p) d"), ot[:, j, :]).then_inc(s_out[j], 16)
            for j in range(2):
                sp.wait_ge(s_out[j], NT // 2 * 16)

        @block.gpsimd
        def _(pool):
            pool.memset(ones[:, :], 1.0).then_inc(s_mean, 1)

            def lower(n, src, j):
                pool.wait_ge(s_ahi, n + 1)
                pool.tensor_tensor(a_lo[:, j], src, a_hi[:, j].bitcast(F32), ALU.subtract).then_inc(s_alo, 1)

            for b in range(z.B):
                with pool.Fori(0, TILES // 2) as m:
                    for j in range(2):
                        lower(b * TILES + 2 * m + j, attn_tile(b, 2 * m + j), j)
                if b == 0:
                    for k in range(ER):
                        pool.wait_ge(s_hi, z.DC + k + 1)
                        pool.tensor_tensor(dn_lo[:, k], c["down"][:, k], dn_hi[:, k].bitcast(F32),
                                           ALU.subtract).then_inc(s_dlo, 1)
            for b in range(z.B):
                with pool.Fori(0, TILES // 2) as m:
                    for j in range(2):
                        lower(NT + b * TILES + 2 * m + j, xt_tile(b, 2 * m + j), j)

        @block.scalar
        def _(act):
            for k in range(z.DC):
                act.copy(wo_hi[:, k], c["wo"][:, k]).then_inc(s_hi, 1)

            def first_tiles(b, m):
                for j in range(2):
                    n = b * TILES + 2 * m + j
                    wait(act, s_y, n - 1)
                    act.copy(a_hi[:, j], attn_tile(b, 2 * m + j)).then_inc(s_ahi, 1)
                for j in range(2):
                    n = b * TILES + 2 * m + j
                    wait(act, s_ln, LN_STEPS * n + 3)
                    act.activation(small[:, j, 1:2], small[:, j, 0:1], ACT.Sqrt).then_inc(s_sqrt, 1)
                for j in range(2):
                    n = b * TILES + 2 * m + j
                    wait(act, s_tr, n + 1)
                    act.copy(xt_tile(b, 2 * m + j), pt[:, j]).then_inc(s_xt, 1)

            pairs(act, 0, first_tiles)
            for k in range(ER):
                act.copy(dn_hi[:, k], c["down"][:, k]).then_inc(s_hi, 1)
            pairs(act, 1, first_tiles)

            def last_tiles(b, m):
                for j in range(2):
                    n = b * TILES + 2 * m + j
                    wait(act, s_zp, n - 1)
                    act.copy(a_hi[:, j], xt_tile(b, 2 * m + j)).then_inc(s_ahi, 1)

            act.wait_ge(s_y, NT)
            act.wait_ge(s_gv, 3)
            act.activation(soft[:, 1], soft[:, 0], ACT.Exp, bias=soft[:, 3, 0:1], scale=KEY ** -0.5,
                           accum_out=soft[:, 3, 1:2]).then_inc(s_ge, 1)
            for b in range(z.B):
                for k in range(z.DC):
                    n = b * z.DC + k
                    wait(act, s_sum, n + 1)
                    if k == 0 and b:
                        wait(act, s_zp, b * TILES)
                    act.copy(wf_hi[:, k], wsum[:, k]).then_inc(s_whi, 1)
                pairs(act, b, last_tiles)

        @block.vector
        def _(dve):
            for k in range(z.DC):
                wait(dve, s_hi, k + 1)
                dve.tensor_tensor(wo_lo[:, k], c["wo"][:, k], wo_hi[:, k].bitcast(F32), ALU.subtract).then_inc(s_lo, 1)

            def tile_ln(b, m, j):
                n = b * TILES + 2 * m + j
                base = LN_STEPS * n
                row = res[:, bass.ds(n, 1), :].rearrange("p a d -> p (a d)")
                wait(dve, s_y, n + 1)
                dve.tensor_tensor(row, py[:, j, :], row, ALU.add).then_inc(s_res, 1)
                wait(dve, s_res, n + 1, apart=True)
                dve.bn_stats(stats[:, j, :], row).then_inc(s_ln, 1)
                wait(dve, s_ln, base + 1, apart=True)
                dve.bn_aggr(mv[:, j, :], stats[:, j, :]).then_inc(s_ln, 1)
                wait(dve, s_ln, base + 2)
                dve.tensor_scalar(small[:, j, 0:1], mv[:, j, 1:2], EPS, None, ALU.add).then_inc(s_ln, 1)
                return row

            def tile_norm(b, m, j):
                n = b * TILES + 2 * m + j
                row = res[:, bass.ds(n, 1), :].rearrange("p a d -> p (a d)")
                part = [small[:, j, q:q + 1] for q in range(4)]
                rsqrt_newton(dve, part, s_root, ROOT_STEPS * n, s_sqrt, n + 1)
                wait(dve, s_tr, n - 1)
                dve.tensor_scalar(xn[:, j, :], row, mv[:, j, 0:1], part[3], ALU.subtract, ALU.mult).then_inc(s_xn, 1)

            def first_tiles(b, m):
                for j in range(2):
                    tile_ln(b, m, j)
                for j in range(2):
                    tile_norm(b, m, j)

            def mean_of(b):
                wait(dve, s_xt, TILES * (b + 1))
                dve.reduce_sum(mean[:, b * z.DC:(b + 1) * z.DC], xt[:, b * z.DC:(b + 1) * z.DC, :], AX.X).then_inc(s_mean, 1)

            dve.wait_ge(s_x[0], 16)
            pairs(dve, 0, first_tiles)
            dve.wait_ge(s_x[1], 16)
            pairs(dve, 1, first_tiles, between=lambda: mean_of(0))
            mean_of(1)
            dve.wait_ge(s_gate, 1)
            dve.tensor_scalar(gate_q[:, :], pg[:, 0, 0:z.B], 1.0 / z.S, None, ALU.mult).then_inc(s_gv, 1)
            dve.wait_ge(s_gate, 2)
            dve.tensor_copy(soft[:, 0], pg[0:z.B, 1, 0:EXPERTS])
            dve.reduce_max(soft[:, 2, 0:1], pg[0:z.B, 1, 0:EXPERTS], AX.X).then_inc(s_gv, 1)
            dve.wait_ge(s_gv, 2)
            dve.tensor_scalar(soft[:, 3, 0:1], soft[:, 2, 0:1], -KEY ** -0.5, None, ALU.mult).then_inc(s_gv, 1)
            dve.wait_ge(s_ge, 1)
            dve.reciprocal(soft[:, 3, 2:3], soft[:, 3, 1:2]).then_inc(s_gv, 1)
            dve.wait_ge(s_gv, 4)
            dve.tensor_scalar(soft[:, 2], soft[:, 1], soft[:, 3, 2:3], None, ALU.mult).then_inc(s_gv, 1)
            dve.wait_ge(s_gv, 5)
            for b in range(z.B):
                dve.tensor_scalar(spread[:, b], soft[:, 2], c["ident"][0:z.B, b:b + 1], None, ALU.mult).then_inc(s_gv, 1)
            dve.wait_ge(s_gate, 3)
            every = pg[:, 0, 0:z.B * EXPERTS].rearrange("p (b k r) -> p b k r", b=z.B, r=2)
            for half in range(2):
                rows = slice(RANK * half, RANK * (half + 1))
                dve.tensor_copy(coeff[rows, :, :], every[rows, :, :, half]).then_inc(s_gv, 1)
            dve.wait_ge(s_gv, 9)

            def scale_up(b):
                wait(dve, s_eff, b * z.DC)
                for k in range(ER):
                    dve.tensor_scalar(up_hi[:, k], c["up"][:, k], coeff[:, b, k:k + 1], None, ALU.mult).then_inc(s_uhi, 1)
                    wait(dve, s_uhi, b * ER + k + 1)
                    dve.scalar_tensor_tensor(out=up_lo[:, k], in0=c["up"][:, k], scalar=coeff[:, b, k:k + 1],
                                             in1=up_hi[:, k].bitcast(F32), op0=ALU.mult, op1=ALU.subtract).then_inc(s_ulo, 1)

            def effective(b):
                for k in range(z.DC):
                    n = b * z.DC + k
                    wait(dve, s_eff, n + 1)
                    dve.tensor_tensor(wsum[:, k], pw[:, k % 2, :], c["w_org"][:, k], ALU.add).then_inc(s_sum, 1)
                    wait(dve, s_whi, n + 1)
                    dve.tensor_tensor(wf_lo[:, k], wsum[:, k], wf_hi[:, k].bitcast(F32), ALU.subtract).then_inc(s_wlo, 1)

            def last_tiles(b, m):
                for j in range(2):
                    n = b * TILES + 2 * m + j
                    wait(dve, s_zp, n + 1)
                    wait(dve, s_out[j], (b * (TILES // 2) + m) * 16)
                    dve.tensor_tensor(ot[:, j, :], py[:, j, :], res[:, bass.ds(n, 1), :].rearrange("p a d -> p (a d)"),
                                      ALU.add).then_inc(s_o, 1)

            scale_up(0)
            effective(0)
            scale_up(1)
            pairs(dve, 0, last_tiles)
            effective(1)
            pairs(dve, 1, last_tiles)

        @block.tensor
        def _(pe):
            def first_tiles(b, m):
                for j in range(2):
                    n = b * TILES + 2 * m + j
                    wait(pe, s_alo, n + 1)
                    wait(pe, s_res, n - 1)
                    for k in range(z.DC):
                        mm = exact_product(pe, py[:, j, :], a_hi[:, j, k], a_lo[:, j, k], wo_hi[:, k], wo_lo[:, k],
                                           k == 0, k == z.DC - 1)
                    mm.then_inc(s_y, 1)
                for j in range(2):
                    n = b * TILES + 2 * m + j
                    wait(pe, s_xn, n + 1)
                    wait(pe, s_xt, n - 1)
                    for k in range(z.DC):
                        mm = pe.transpose(pt[:, j, k, :], xn[:, j, k * P:(k + 1) * P], c["ident"][:, :])
                    mm.then_inc(s_tr, 1)

            def last_tiles(b, m):
                for j in range(2):
                    n = b * TILES + 2 * m + j
                    wait(pe, s_alo, NT + n + 1)
                    wait(pe, s_o, n - 1)
                    for k in range(z.DC):
                        mm = exact_product(pe, py[:, j, :], a_hi[:, j, k], a_lo[:, j, k], wf_hi[:, k], wf_lo[:, k],
                                           k == 0, k == z.DC - 1)
                    mm.then_inc(s_zp, 1)

            pe.wait_ge(s_lo, z.DC)
            for b in range(z.B):
                pairs(pe, b, first_tiles)
            pe.wait_ge(s_mean, 1 + z.B)
            for k in range(z.DC):
                mm = pe.matmul(pg[:, 0, 0:z.B], c["wq"][:, k, :], mean[:, :].rearrange("p (b k) -> p k b", b=z.B)[:, k, :],
                               start=(k == 0), stop=(k == z.DC - 1))
            mm.then_inc(s_gate, 1)
            pe.wait_ge(s_gv, 1)
            pe.matmul(pg[0:z.B, 1, 0:EXPERTS], gate_q[:, :], c["keys"][:, :], start=True, stop=True).then_inc(s_gate, 1)
            pe.wait_ge(s_gv, 7)
            pe.matmul(pg[:, 0, 0:z.B * EXPERTS], ones[:, :], spread[:, :, :].rearrange("p b e -> p (b e)"),
                      start=True, stop=True).then_inc(s_gate, 1)
            for b in range(z.B):
                wait(pe, s_dlo, ER)
                for k in range(z.DC):
                    n = b * z.DC + k
                    wait(pe, s_sum, n - 1)
                    for r in range(ER):
                        if k == 0:
                            wait(pe, s_ulo, b * ER + r + 1)
                        cols = slice(k * P, (k + 1) * P)
                        mm = exact_product(pe, pw[:, k % 2, :], dn_hi[:, r, cols], dn_lo[:, r, cols],
                                           up_hi[:, r], up_lo[:, r], r == 0, r == ER - 1)
                    mm.then_inc(s_eff, 1)
                wait(pe, s_wlo, (b + 1) * z.DC)
                pairs(pe, b, last_tiles)



def _rotation_tables(z):
    import numpy as np
    inv = (1.0 / np.float32(THETA) ** (np.arange(0, z.HD, 2, dtype=np.float32) / np.float32(z.HD))).astype(np.float32)
    angle = np.arange(z.S, dtype=np.float32)[:, None] * inv[None, :]
    both = np.stack([np.cos(angle), np.sin(angle)]).astype(np.float32)
    rows = np.tile(np.repeat(both.transpose(2, 0, 1), z.GH, axis=0), (4, 1, 1))
    chunks = rows.reshape(P, 2, z.NC, z.CT).transpose(2, 0, 1, 3)
    return np.ascontiguousarray(np.repeat(chunks, z.B, axis=0))


def kernel(L0_attn_hidden_states, L0_attn_wq, L0_attn_wk, L0_attn_wv, L0_attn_wo, L0_ffn_W_org,
           L0_ffn_lora_down, L0_ffn_lora_up, L0_ffn_lora_keys, L0_ffn_Wq):
    import numpy as np
    import concourse.bacc as bacc
    from concourse.bass_utils import run_bass_kernel_spmd

    x = np.asarray(L0_attn_hidden_states)
    z = Sizes(*x.shape)

    def by_half(w):
        w = np.asarray(w).reshape(z.D, z.SG, 4, z.GH, 2, z.HALF)
        return w.transpose(0, 1, 4, 2, 5, 3).reshape(z.D, z.D)

    arrays = {
        "x": x,
        "xc": x.reshape(z.B, z.NC, z.CT, z.D).transpose(1, 0, 2, 3).reshape(z.CHUNKS, z.CT, z.D),
        "w_in": np.concatenate([by_half(L0_attn_wq), by_half(L0_attn_wk), np.asarray(L0_attn_wv)], axis=1),
        "rope": _rotation_tables(z),
        "w_o": np.asarray(L0_attn_wo),
        "w_org_t": np.asarray(L0_ffn_W_org).T,
        "down_t": np.asarray(L0_ffn_lora_down).transpose(0, 2, 1).reshape(EXPERTS * RANK, z.D),
        "up": np.asarray(L0_ffn_lora_up).reshape(EXPERTS * RANK, z.D),
        "keys_t": np.asarray(L0_ffn_lora_keys).T,
        "wq_t": np.asarray(L0_ffn_Wq).T,
    }
    arrays = {n: np.ascontiguousarray(a) for n, a in arrays.items()}
    nc = bacc.Bacc("TRN2", target_bir_lowering=False, num_devices=1)
    args = [nc.dram_tensor("in_" + n, a.shape, mybir.dt.from_np(a.dtype), kind="ExternalInput").ap() for n, a in arrays.items()]
    args.append(nc.dram_tensor("y", x.shape, F32, kind="ExternalOutput").ap())
    layer_kernel(nc, *args)
    result = run_bass_kernel_spmd(nc, [{"in_" + n: a for n, a in arrays.items()}], core_ids=[0])
    return result.results[0]["y"]
```

```python
from contextlib import ExitStack

import concourse.bass as bass
from concourse import mybir

ALU = mybir.AluOpType
ACT = mybir.ActivationFunctionType
AX = mybir.AxisListType
F32 = mybir.dt.float32
F32R = mybir.dt.float32r
BF16 = mybir.dt.bfloat16

P = 128
HEADS = 32
THETA = 10000.0
EPS = 1e-5
EXPERTS, RANK, KEY = 8, 64, 128


def wait(eng, sem, value, apart=False):
    if isinstance(value, int):
        if value > 0:
            eng.wait_ge(sem, value)
        return
    eng.wait_ge(sem, value)
    if apart:
        eng.nop(nofuse=True)


class Sizes:

    def __init__(s, batches, seq, dim):
        s.B, s.S, s.D = batches, seq, dim
        s.HD = dim // HEADS
        s.HALF = s.HD // 2
        s.DC = dim // P
        s.CT = 512
        s.NC = seq // s.CT
        s.TT = s.CT // P
        s.CHUNKS = batches * s.NC
        s.SG = HEADS // 16
        s.GH = 4
        s.GB = HEADS // s.GH
        s.G = batches * s.GB
        s.KT = seq // P
        s.ROWS = 6 * s.HD


Q_RUNS = [(0, 3), (0, 2), (0, 1)]
K_PARTS = [(0, 3), (1, 2), (2, 1)]


def layer_kernel(nc, x, xc, w_in, rope, w_o, w_org_t, down_t, up, keys_t, wq_t, out):
    z = Sizes(*x.shape)
    scratch = {n: nc.dram_tensor(f"{n}_parts", [z.NC * z.G, 3, 2, z.HALF, z.GH, z.CT], BF16,
                                 kind="Internal").ap() for n in "qk"}
    with ExitStack() as keep:
        def sb(name, shape, dt):
            return keep.enter_context(nc.sbuf_tensor(name, shape, dt))

        def sem(name):
            return keep.enter_context(nc.semaphore(name))

        c = {
            "ident": sb("ident", [P, P], F32),
            "ident_b": sb("ident_b", [P, P], BF16),
            "causal": sb("causal", [P, P], BF16),
            "wo": sb("wo", [P, z.DC, z.D], F32),
            "w_org": sb("w_org", [P, z.DC, z.D], F32),
            "down": sb("down", [P, z.DC, z.D], F32),
            "up": sb("up", [P, z.DC, z.D], F32),
            "wq": sb("wq_gate", [P, z.DC, KEY], F32),
            "keys": sb("keys", [KEY, EXPERTS], F32),
            "s_weights": sem("weights_loaded"),
            "s_const": sem("constants_ready"),
        }
        values = sb("values", [P, z.NC, z.G, z.TT, z.GH * z.HD], F32)
        project_phase(nc, z, c, xc, w_in, rope, (w_o, w_org_t, down_t, up, keys_t, wq_t), scratch, values)
        attn_t = sb("attn_t", [P, z.B * z.DC, z.S], F32)
        attention_phase(nc, z, c, scratch, values, attn_t)
        ffn_phase(nc, z, c, x, values, attn_t, out)



def project_phase(nc, z, c, xc, w_in, rope, weights, scratch, values):
    NU = 2 * z.SG
    QKC = 2 * z.D
    with ExitStack() as ctx:
        def sb(name, shape, dt):
            return ctx.enter_context(nc.sbuf_tensor(name, shape, dt))

        def sem(name):
            return ctx.enter_context(nc.semaphore(name))

        wraw = sb("wraw", [P, 3 * z.D], F32)
        whi = sb("whi", [P, z.DC, 3 * z.D], F32R)
        wlo = sb("wlo", [P, z.DC, 3 * z.D], F32R)
        xin = sb("xin", [P, z.TT, z.D], F32)
        xn = sb("xn", [P, z.TT, z.D], F32)
        xhi = sb("xhi", [P, z.DC, z.CT], F32R)
        xlo = sb("xlo", [P, z.DC, z.CT], F32R)
        table = sb("table", [P, 2, z.CT], F32)
        prod = sb("prod", [P, 2, 4, z.CT], F32)
        rot = sb("rot", [P, 2, 2, z.CT], F32)
        rest = sb("rest", [P, 2, z.CT], F32)
        parts = sb("parts", [P, 2, 3, 2, z.CT], BF16)
        stats = sb("stats", [P, z.TT, 6], F32)
        mv = sb("mv", [P, z.TT, 2], F32)
        small = sb("small", [P, 4, z.TT], F32)

        pt = ctx.enter_context(nc.psum_tensor("pt", [P, 2, z.DC, P], F32))
        pu = ctx.enter_context(nc.psum_tensor("pu", [P, 2, 2, z.CT], F32))
        pv = ctx.enter_context(nc.psum_tensor("pv", [P, 2, z.D], F32))

        s_wraw = sem("wraw_loaded")
        s_whi = sem("whi_ready")
        s_wlo = sem("wlo_ready")
        s_x = sem("x_loaded")
        s_table = sem("table_loaded")
        s_ln = sem("ln_small")
        s_sqrt = sem("sqrt_ready")
        s_xn = sem("xn_ready")
        s_tr = sem("transposed")
        s_xhi = sem("xhi_ready")
        s_xlo = sem("xlo_ready")
        s_unit = sem("unit_projected")
        s_v = sem("v_projected")
        s_vout = sem("v_stored")
        s_prod = sem("products_ready")
        s_rot = sem("rotated")
        s_p1 = sem("part1_ready")
        s_rest = sem("rest_ready")
        s_p2 = sem("part2_ready")
        s_p3 = sem("part3_ready")
        s_put = [sem("parts_stored_even"), sem("parts_stored_odd")]
        s_setup = sem("pool_setup")

        LN_STEPS = 6 + 2
        block = ctx.enter_context(nc.Block())

        @block.sync
        def _(sp):
            def load_x(i):
                wait(sp, s_xn, z.TT * i)
                sp.dma_start(xin[:, :, :], xc[bass.ds(i, 1)].rearrange("a (t p) d -> p (a t) d", p=P)).then_inc(s_x, 16)

            def load_table(i):
                wait(sp, s_prod, NU * 2 * i)
                sp.dma_start(table[:, :, :], rope[bass.ds(i, 1)].rearrange("a p s t -> p (a s) t")).then_inc(s_table, 16)

            def store_parts(i):
                for u in range(NU):
                    to = scratch["qk"[u // z.SG]]
                    g = u % z.SG
                    wait(sp, s_p3, NU * i + u + 1)
                    for part in range(3):
                        for half in range(2):
                            dst = to[bass.ds(i * z.GB + g * z.GH, z.GH), part, half].rearrange("g e h t -> g (e h) t")
                            sp.dma_start(dst, parts[:, u % 2, part, half, :]).then_inc(s_put[u % 2], 16)

            load_x(0)
            for kc in range(z.DC):
                wait(sp, s_wlo, kc)
                sp.dma_start(wraw[:, :], w_in[kc * P:(kc + 1) * P, :]).then_inc(s_wraw, 16)
            load_table(0)
            w_o, w_org_t, down_t, up, keys_t, wq_t = weights
            with sp.Fori(0, z.CHUNKS - 1) as i:
                load_x(i + 1)
                store_parts(i)
                load_table(i + 1)
            for name, src in (("wo", w_o), ("w_org", w_org_t), ("down", down_t), ("up", up), ("wq", wq_t)):
                sp.dma_start(c[name][:, :, :], src.rearrange("(a p) n -> p a n", p=P)).then_inc(c["s_weights"], 16)
            sp.dma_start(c["keys"][:, :], keys_t).then_inc(c["s_weights"], 16)
            store_parts(z.CHUNKS - 1)
            for par in range(2):
                sp.wait_ge(s_put[par], z.CHUNKS * NU // 2 * 6 * 16)
            sp.wait_ge(c["s_weights"], 6 * 16)

        @block.gpsimd
        def _(pool):
            pool.memset(c["ident"][:, :], 0.0).then_inc(s_setup, 1)
            pool.memset(c["ident_b"][:, :], 0.0).then_inc(s_setup, 1)
            pool.memset(c["causal"][:, :], 0.0).then_inc(s_setup, 1)
            pool.wait_ge(s_setup, 3)
            for m in (c["ident"], c["ident_b"]):
                pool.affine_select(out=m[:, :], in_=m[:, :], compare_op=ALU.not_equal, fill=1.0, base=0,
                                   pattern=[[-1, P]], channel_multiplier=1).then_inc(c["s_const"], 1)
            pool.affine_select(out=c["causal"][:, :], in_=c["causal"][:, :], compare_op=ALU.is_ge, fill=-3e38,
                               base=0, pattern=[[-1, P]], channel_multiplier=1).then_inc(c["s_const"], 1)

            def rotate(i):
                for u in range(NU):
                    n = NU * i + u
                    pr, ro = prod[:, u % 2], rot[:, u % 2]
                    wait(pool, s_rest, n - 1)
                    wait(pool, s_prod, 2 * n + 1)
                    pool.tensor_tensor(ro[:, 0], pr[:, 0], pr[:, 1], ALU.subtract).then_inc(s_rot, 1)
                    wait(pool, s_prod, 2 * n + 2)
                    pool.tensor_tensor(ro[:, 1], pr[:, 2], pr[:, 3], ALU.add).then_inc(s_rot, 1)

            rotate(0)
            with pool.Fori(1, z.CHUNKS) as i:
                rotate(i)

        @block.scalar
        def _(act):
            def root(i):
                wait(act, s_ln, LN_STEPS * i + 3)
                act.activation(small[:, 1], small[:, 0], ACT.Sqrt).then_inc(s_sqrt, 1)

            def upper(i):
                wait(act, s_v, z.TT * i)
                for t in range(z.TT):
                    wait(act, s_tr, z.TT * i + t + 1)
                    act.copy(xhi[:, :, t * P:(t + 1) * P], pt[:, t % 2]).then_inc(s_xhi, 1)

            def parts12(i, u):
                n = NU * i + u
                wait(act, s_put[u % 2], (i * (NU // 2) + u // 2) * 96)
                wait(act, s_rot, 2 * n + 2)
                act.copy(parts[:, u % 2, 0], rot[:, u % 2]).then_inc(s_p1, 1)
                wait(act, s_rest, n + 1)
                act.copy(parts[:, u % 2, 1], rest[:, :, :]).then_inc(s_p2, 1)

            def store_v(i):
                for t in range(z.TT):
                    wait(act, s_v, z.TT * i + t + 1)
                    act.copy(values[:, :, :, :, :].rearrange("p n g t f -> p (n g) t f")[:, bass.ds(i * z.GB, z.GB), t, :],
                             pv[:, t % 2].rearrange("p (g f) -> p g f", g=z.GB)).then_inc(s_vout, 1)

            act.wait_ge(s_wraw, 16)
            for kc in range(z.DC):
                wait(act, s_wraw, 16 * (kc + 1))
                act.copy(whi[:, kc], wraw[:, :]).then_inc(s_whi, 1)
                if kc == 0:
                    root(0)
            upper(0)

            def body(i):
                for u in range(NU):
                    parts12(i, u)
                    if u == 2:
                        root(i + 1)
                store_v(i)
                upper(i + 1)

            body(0)
            with act.Fori(1, z.CHUNKS - 1) as i:
                body(i)
            for u in range(NU):
                parts12(z.CHUNKS - 1, u)
            store_v(z.CHUNKS - 1)

        @block.vector
        def _(dve):
            def ln_stats(i):
                base = LN_STEPS * i
                wait(dve, s_x, 16 * (i + 1), apart=True)
                for t in range(z.TT):
                    ins = dve.bn_stats(stats[:, t, :], xin[:, t, :])
                ins.then_inc(s_ln, 1)
                wait(dve, s_ln, base + 1, apart=True)
                for t in range(z.TT):
                    ins = dve.bn_aggr(mv[:, t, :], stats[:, t, :])
                ins.then_inc(s_ln, 1)
                wait(dve, s_ln, base + 2)
                dve.tensor_scalar(small[:, 0], mv[:, :, 1], EPS, None, ALU.add).then_inc(s_ln, 1)

            def ln_apply(i):
                rsqrt_newton(dve, [small[:, n] for n in range(4)], s_ln, LN_STEPS * i + 3, s_sqrt, i + 1)
                wait(dve, s_tr, z.TT * i)
                for t in range(z.TT):
                    dve.tensor_scalar(xn[:, t, :], xin[:, t, :], mv[:, t, 0:1], small[:, 3, t:t + 1],
                                      ALU.subtract, ALU.mult).then_inc(s_xn, 1)

            def lower(i):
                for t in range(z.TT):
                    wait(dve, s_xhi, z.TT * i + t + 1)
                    hi = xhi[:, :, t * P:(t + 1) * P]
                    dve.tensor_tensor(xlo[:, :, t * P:(t + 1) * P], pt[:, t % 2], hi.bitcast(F32),
                                      ALU.subtract).then_inc(s_xlo, 1)

            def products(i, u, half):
                n = NU * i + u
                a, b = pu[:, u % 2, 0, :], pu[:, u % 2, 1, :]
                if half == 0:
                    wait(dve, s_unit, n + 1)
                    wait(dve, s_rot, 2 * n - 2)
                    dve.tensor_tensor(prod[:, u % 2, 0], a, table[:, 0], ALU.mult)
                    dve.tensor_tensor(prod[:, u % 2, 1], b, table[:, 1], ALU.mult).then_inc(s_prod, 1)
                else:
                    dve.tensor_tensor(prod[:, u % 2, 2], b, table[:, 0], ALU.mult)
                    dve.tensor_tensor(prod[:, u % 2, 3], a, table[:, 1], ALU.mult).then_inc(s_prod, 1)

            def rest_of(i, u):
                n = NU * i + u
                wait(dve, s_p3, n)
                wait(dve, s_p1, n + 1)
                dve.tensor_tensor(rest[:, :, :], rot[:, u % 2], parts[:, u % 2, 0], ALU.subtract).then_inc(s_rest, 1)

            def part3(i, u):
                n = NU * i + u
                wait(dve, s_p2, n + 1)
                dve.tensor_tensor(parts[:, u % 2, 2], rest[:, :, :], parts[:, u % 2, 1], ALU.subtract).then_inc(s_p3, 1)

            def units(i, more):
                wait(dve, s_table, 16 * (i + 1))
                for u in range(NU):
                    products(i, u, 0)
                    if u:
                        rest_of(i, u - 1)
                    products(i, u, 1)
                    if u:
                        part3(i, u - 1)
                    if u == 1 and more:
                        ln_stats(i + 1)
                rest_of(i, NU - 1)
                if more:
                    ln_apply(i + 1)
                part3(i, NU - 1)

            ln_stats(0)
            ln_apply(0)
            for kc in range(z.DC):
                wait(dve, s_whi, kc + 1)
                dve.tensor_tensor(wlo[:, kc], wraw[:, :], whi[:, kc].bitcast(F32), ALU.subtract).then_inc(s_wlo, 1)
            lower(0)
            units(0, True)
            with dve.Fori(1, z.CHUNKS - 1) as i:
                wait(dve, s_v, z.TT * i)
                lower(i)
                units(i, True)
            wait(dve, s_v, z.TT * (z.CHUNKS - 1))
            lower(z.CHUNKS - 1)
            units(z.CHUNKS - 1, False)

        @block.tensor
        def _(pe):
            pe.wait_ge(c["s_const"], 3)

            def transposes(i):
                for t in range(z.TT):
                    wait(pe, s_xn, z.TT * i + t + 1)
                    wait(pe, s_xlo, z.TT * i + t - 1)
                    for k in range(z.DC):
                        mm = pe.transpose(pt[:, t % 2, k, :], xn[:, t, k * P:(k + 1) * P], c["ident"][:, :])
                    mm.then_inc(s_tr, 1)

            def project(i):
                wait(pe, s_xlo, z.TT * (i + 1))
                for u in range(NU):
                    n = NU * i + u
                    wait(pe, s_prod, 2 * n - 2)
                    for half in range(2):
                        col = slice(u * 256 + half * P, u * 256 + (half + 1) * P)
                        for k in range(z.DC):
                            if half == 0 and u == 0 and isinstance(i, int) and i == 0:
                                wait(pe, s_wlo, k + 1)
                            mm = exact_product(pe, pu[:, u % 2, half, :], whi[:, k, col], wlo[:, k, col],
                                               xhi[:, k, :], xlo[:, k, :], k == 0, k == z.DC - 1)
                    mm.then_inc(s_unit, 1)
                for t in range(z.TT):
                    wait(pe, s_vout, z.TT * i + t - 1)
                    tok = slice(t * P, (t + 1) * P)
                    for k in range(z.DC):
                        mm = exact_product(pe, pv[:, t % 2, :], xhi[:, k, tok], xlo[:, k, tok],
                                           whi[:, k, QKC:], wlo[:, k, QKC:], k == 0, k == z.DC - 1)
                    mm.then_inc(s_v, 1)

            transposes(0)
            project(0)
            transposes(1)
            with pe.Fori(1, z.CHUNKS - 1) as i:
                project(i)
                transposes(i + 1)
            project(z.CHUNKS - 1)


def exact_product(pe, out, a_hi, a_lo, b_hi, b_lo, first, last):
    pe.matmul(out, a_hi, b_hi, start=first, stop=False)
    pe.matmul(out, a_hi, b_lo, start=False, stop=False)
    return pe.matmul(out, a_lo, b_hi, start=False, stop=last)


def rsqrt_newton(dve, small, s_step, base, s_sqrt, roots):
    v, s0, t, r = small
    wait(dve, s_sqrt, roots)
    dve.reciprocal(t, s0).then_inc(s_step, 1)
    wait(dve, s_step, base + 1)
    dve.tensor_tensor(t, t, v, ALU.mult).then_inc(s_step, 1)
    wait(dve, s_step, base + 2)
    dve.tensor_tensor(t, t, s0, ALU.add).then_inc(s_step, 1)
    wait(dve, s_step, base + 3)
    dve.reciprocal(r, t).then_inc(s_step, 1)
    wait(dve, s_step, base + 4)
    dve.tensor_scalar(r, r, 2.0, None, ALU.mult).then_inc(s_step, 1)
    wait(dve, s_step, base + 5)



def attention_phase(nc, z, c, scratch, values, attn_t):
    STEPS = [(qc, kb) for qc in range(z.NC) for kb in range(z.TT * (qc + 1))]
    NS = len(STEPS)
    RING = 3
    LAG = 2
    QT, HG = z.TT, z.GH
    MP = 2
    MROWS = MP * HG * QT

    tiles = []
    for qc in range(z.NC):
        for qt in range(QT):
            for kc in range(qc + 1):
                width = z.CT if kc < qc else (qt + 1) * P
                n = z.CT // width
                tiles.append([(qc, qt, kc, width, h, min(n, HG - h)) for h in range(0, HG, n)])
    chunk_tiles = [sum(tiles[:QT], []), sum(tiles[QT:], [])]
    T0, AFTER = len(chunk_tiles[0]), 4
    ITEMS = [(1, t) for t in chunk_tiles[0]]
    ITEMS.insert(4, (0, "turn 1"))
    ITEMS += [(1, t) for t in chunk_tiles[1][:AFTER]] + [(1, "turn 0")] + [(1, t) for t in chunk_tiles[1][AFTER:]]
    NI = len(ITEMS)
    TURN = {1: 4, 0: T0 + 1 + AFTER}
    SLOTS = [0, 4, 8, 10, 12, 17, 21, 25, 29, 33, 36, 38, NI]
    assert NI % 2 == 0 and ITEMS[TURN[0]][1] == "turn 0"
    MASKED = [s for s, (qc, kb) in enumerate(STEPS) if kb >= z.TT * qc]

    def q0(step):
        qc, kb = STEPS[step]
        return max(0, kb - z.TT * qc) * P

    with ExitStack() as ctx:
        def sb(name, shape, dt):
            return ctx.enter_context(nc.sbuf_tensor(name, shape, dt))

        def sem(name):
            return ctx.enter_context(nc.semaphore(name))

        qs = [sb(f"q_stack{n}", [P, z.NC, HG, z.CT], BF16) for n in range(2)]
        ks = [sb(f"k_stack{n}", [P, z.NC, HG, z.CT], BF16) for n in range(2)]
        probs = [sb(f"probs{n}", [P, HG, z.CT], F32) for n in range(RING)]
        vg = [sb(f"v_group{n}", [P, z.KT, HG, 2 * z.HD], F32) for n in range(2)]
        raw = sb("out_raw", [P, z.NC, z.CT], F32)
        sums = sb("sums", [P, HG * z.S // P], F32)
        num = sb("numerator", [P, z.S], F32)
        inv = sb("inverse_sums", [P, z.S], F32)
        top = sb("row_max", [P, 2, z.NC, HG, QT], F32)
        top2 = sb("row_max_late", [P, 2, HG, QT], F32)
        neg = sb("neg_parts", [P, z.NC, MP, HG, QT], BF16)
        rows = [sb(f"neg_rows{n}", [MROWS, P], BF16) for n in range(z.NC)]

        st = [ctx.enter_context(nc.psum_tensor(f"scores_t{n}", [P, 2, z.CT], F32)) for n in range(2)]
        po = [ctx.enter_context(nc.psum_tensor(f"out_t{n}", [P, z.CT], F32)) for n in range(z.NC)]
        pm = [ctx.enter_context(nc.psum_tensor(f"max_bank{n}", [P, z.CT], F32)) for n in range(2)]

        s_ones = sem("ones_ready")
        s_stack = [[sem(f"stack_loaded{n}_{qc}") for qc in range(z.NC)] for n in range(2)]
        s_item = sem("max_bank_filled")
        s_taken = sem("max_bank_read")
        s_comb = sem("max_combined")
        s_neg = sem("neg_steps")
        s_rows = [sem(f"neg_rows_loaded{n}") for n in range(z.NC)]
        s_qk = sem("scores_ready")
        s_exp = sem("exp_done")
        s_mask = sem("masked")
        s_pv = sem("pv_done")
        s_vg = sem("v_group_ready")
        s_raw = sem("out_raw_ready")
        s_bounce = sem("out_in_dram")
        s_num = sem("numerator_loaded")
        s_sums = sem("sums_loaded")
        s_inv = sem("reciprocal_ready")
        s_back = sem("reciprocal_in_dram")
        s_spread = sem("reciprocal_spread")
        s_free = sem("numerator_free")

        ITERS = z.G // 2
        LOADS = len(Q_RUNS) + len(K_PARTS)

        bounce = nc.dram_tensor("out_by_group", [z.G, HG, 2 * z.HD, z.S], F32, kind="Internal").ap()
        inverse = nc.dram_tensor("inverse_by_group", [z.G, HG, z.S], F32, kind="Internal").ap()

        block = ctx.enter_context(nc.Block())

        def turned(g, qc, last):
            if last:
                return NI * (g + 1) + 1
            return NI * (g + 1 - (1 - qc)) + TURN[qc] + 1

        def ring(g, last, lo, hi):
            if last:
                return [(NI * (g + 1), 0, (0, "turn 1"))] if lo <= TURN[1] < hi else []
            return [(NI * (g + 1) + n, n % 2, (ITEMS[n][0], ITEMS[n][1])) for n in range(lo, hi)]

        def run(eng, body):
            body(0, True, False)
            with eng.Fori(1, ITERS - 1) as it:
                body(it, False, False)
            body(ITERS - 1, False, True)

        @block.sync
        def _(sp):
            def load_stacks(g, par, tc):
                last_reader = NS - 1 if tc else NS - 1 - z.TT
                wait(sp, s_qk, 2 * (NS * (g - 2) + last_reader + 1), apart=True)
                own_q, own_k = (scratch[n][bass.ds(g + tc * z.G, 1)].rearrange("g s f e h t -> (g s f e) (h t)")
                                for n in "qk")
                row = 0
                for part, n in Q_RUNS:
                    sp.dma_start(qs[par][row:row + z.HD * n, tc].rearrange("p h t -> p (h t)"),
                                 own_q[z.HD * part:z.HD * (part + n)]).then_inc(s_stack[par][tc], 16)
                    row += z.HD * n
                row = 0
                for part, times in K_PARTS:
                    src = own_k[z.HD * part:z.HD * (part + 1)].rearrange("(a p) t -> a p t", a=1)
                    sp.dma_start(ks[par][row:row + z.HD * times, tc].rearrange("p h t -> p (h t)"),
                                 src.broadcast_to([times, z.HD, HG * z.CT])).then_inc(s_stack[par][tc], 16)
                    row += z.HD * times

            def bounce_out(g):
                wait(sp, s_raw, 2 * (g + 1), apart=True)
                sp.dma_start(bounce[bass.ds(g, 1)].rearrange("a h r t -> (a h r) t"),
                             raw[:, :, :].rearrange("p c t -> p (c t)")).then_inc(s_bounce, 16)

            def bounce_in(g, par, it):
                wait(sp, s_bounce, 16 * (g + 1), apart=True)
                wait(sp, s_free, it + 1, apart=True)
                one = bounce[bass.ds(g, 1)].rearrange("a h r t -> (a h) r t")
                sp.dma_start(num[64 * par:64 * par + 64, :], one[:, 0:z.HD, :]).then_inc(s_num, 16)
                wait(sp, s_back, 16 * g, apart=True)
                sp.dma_start(sums[:, :], one[:, z.HD, :].rearrange("h (x y) -> h x y", x=P // HG)).then_inc(s_sums, 16)

            def sums_out(g):
                wait(sp, s_inv, g + 1, apart=True)
                sp.dma_start(inverse[bass.ds(g, 1)].rearrange("a h (x y) -> (a h x) y", x=P // HG),
                             sums[:, :]).then_inc(s_back, 16)

            def sums_in(g, par):
                wait(sp, s_back, 16 * (g + 1), apart=True)
                one = inverse[bass.ds(g, 1)].rearrange("a h t -> h a t").broadcast_to([HG, z.HD, z.S])
                sp.dma_start(inv[64 * par:64 * par + 64, :], one).then_inc(s_spread, 16)

            def body(it, first, last):
                for par in range(2):
                    g = 2 * it + par
                    before = not (first and par == 0)
                    if not (last and par == 1):
                        load_stacks(g + 1, 1 - par, 1)
                    if before:
                        bounce_out(g - 1)
                        bounce_in(g - 1, 1 - par, it if par else it - 1)
                    if not last:
                        load_stacks(g + 2, par, 0)
                    if before:
                        sums_out(g - 1)
                        sums_in(g - 1, 1 - par)

            load_stacks(0, 0, 0)
            load_stacks(0, 0, 1)
            load_stacks(1, 1, 0)
            run(sp, body)
            bounce_out(z.G - 1)
            bounce_in(z.G - 1, 1, ITERS - 1)
            sums_out(z.G - 1)
            sums_in(z.G - 1, 1)
            sp.wait_ge(s_spread, 16 * z.G)

        @block.gpsimd
        def _(pool):
            pool.memset(vg[0][:, :, :, z.HD:], 1.0).then_inc(s_ones, 1)
            pool.memset(vg[1][:, :, :, z.HD:], 1.0).then_inc(s_ones, 1)
            pool.wait_ge(s_ones, 2)
            pool.memset(ks[0][z.ROWS:, :, :, :], 1.0).then_inc(s_ones, 1)
            pool.memset(ks[1][z.ROWS:, :, :, :], 1.0).then_inc(s_ones, 1)
            pool.wait_ge(s_ones, 4)

            def copy_v(g, par):
                wait(pool, s_pv, NS * (g - 1))
                v = values[:, :, :, :, :].rearrange("p c g t f -> p g c (t f)")[:, bass.ds(g, 1)]
                pool.tensor_copy(vg[par][:, :, :, 0:z.HD].rearrange("p (c t) h f -> p c (t h) f", c=z.NC),
                                 v.rearrange("p a c (n f) -> p (a c) n f", f=z.HD)).then_inc(s_vg, 1)

            def mask(g, step):
                wait(pool, s_exp, 2 * (NS * g + step) + 2, apart=True)
                t = probs[step % RING][:, :, 0:P]
                pool.affine_select(out=t, in_=t, compare_op=ALU.is_ge, fill=0.0, base=0,
                                   pattern=[[0, HG], [1, P]], channel_multiplier=-1).then_inc(s_mask, 1)

            def normalize(it):
                wait(pool, s_num, 32 * (it + 1))
                wait(pool, s_spread, 32 * (it + 1))
                pool.tensor_tensor(attn_t[:, bass.ds(it, 1), :].rearrange("p a t -> p (a t)"),
                                   num[:, :], inv[:, :], ALU.mult).then_inc(s_free, 1)

            def body(it, first, last):
                for par in range(2):
                    g = 2 * it + par
                    for step in range(NS):
                        if step in MASKED:
                            mask(g, step)
                        if step == 3 and not (last and par == 1):
                            copy_v(g + 1, 1 - par)
                        if step == 4 and par == 1 and not first:
                            normalize(it - 1)

            pool.sem_inc(s_free, 1)
            copy_v(0, 0)
            run(pool, body)
            normalize(ITERS - 1)

        @block.scalar
        def _(act):
            def exps(g, step):
                n = NS * g + step
                w = z.CT - q0(step)
                wait(act, s_pv, n - RING + 1)
                for pair in range(2):
                    wait(act, s_qk, 2 * n + pair + 1)
                    act.activation(probs[step % RING][:, 2 * pair:2 * pair + 2, 0:w], st[pair][:, :, 0:w],
                                   ACT.Exp, scale=z.HD ** -0.5).then_inc(s_exp, 1)

            def evacuate(g, qc):
                wait(act, s_pv, NS * g + (z.TT if qc == 0 else NS))
                wait(act, s_bounce, 16 * g)
                act.copy(raw[:, qc, :], po[qc][:, :]).then_inc(s_raw, 1)

            def load_rows(g, par, qc, last):
                wait(act, s_taken, turned(g, qc, last))
                act.dma_start(qs[par][z.ROWS:z.ROWS + MP, qc], rows[qc][:, :]).then_inc(s_rows[qc], 16)

            def body(it, first, last):
                for par in range(2):
                    g = 2 * it + par
                    for step in range(NS):
                        exps(g, step)
                        if step == 2:
                            if not (first and par == 0):
                                evacuate(g - 1, 1)
                            load_rows(g, par, 1, last and par == 1)
                        if step == 6:
                            evacuate(g, 0)
                            if not (last and par == 1):
                                load_rows(g + 1, 1 - par, 0, False)

            load_rows(0, 0, 0, False)
            run(act, body)
            evacuate(z.G - 1, 1)

        @block.vector
        def _(dve):
            def negate(g, par, qc):
                base = 2 * (z.NC * g + (0 if qc == 0 else 1))
                m = top[:, par, qc].rearrange("p h t -> p (h t)")
                part = [neg[:, qc, n].rearrange("p h t -> p (h t)") for n in range(MP)]
                dve.tensor_scalar(part[0], m, -1.0, None, ALU.mult).then_inc(s_neg, 1)
                wait(dve, s_neg, base + 1)
                dve.scalar_tensor_tensor(out=part[1], in0=m, scalar=-1.0, in1=part[0],
                                         op0=ALU.mult, op1=ALU.subtract).then_inc(s_neg, 1)

            def take(g, par, last, lo, hi, prologue=False):
                for k, bank, (ahead, item) in ring(g, last, lo, hi):
                    if prologue and item == "turn 1":
                        continue
                    gi, pi = g + ahead, (par + ahead) % 2
                    wait(dve, s_item, k + 1)
                    if item in ("turn 0", "turn 1"):
                        qc = int(item[-1])
                        wait(dve, s_rows[qc], 16 * gi)
                        dve.tensor_copy(rows[qc][:, :], pm[bank][0:MROWS, 0:P // 2].bitcast(BF16)).then_inc(s_taken, 1)
                        continue
                    qc, qt, kc, width, h, n_heads = item
                    to = (top2[:, pi] if kc < qc else top[:, pi, qc])[:, h:h + n_heads, qt]
                    dve.reduce_max(to, pm[bank][:, 0:n_heads * width].rearrange("p (h k) -> p h k", h=n_heads),
                                   AX.X).then_inc(s_taken, 2 if prologue and (k + 1) % NI == TURN[1] else 1)

            def after(g, par, hi):
                gi, pi = g + 1, 1 - par
                if hi == SLOTS[4]:
                    wait(dve, s_taken, NI * gi + hi)
                    negate(gi, pi, 0)
                if hi == NI:
                    wait(dve, s_taken, NI * gi + hi)
                    m = top[:, pi, 1].rearrange("p h t -> p (h t)")
                    dve.tensor_tensor(m, m, top2[:, pi].rearrange("p h t -> p (h t)"), ALU.max).then_inc(s_comb, 1)
                    wait(dve, s_comb, gi + 1)
                    negate(gi, pi, 1)

            def invert(g):
                wait(dve, s_sums, 16 * (g + 1))
                dve.reciprocal(sums[:, :], sums[:, :]).then_inc(s_inv, 1)

            def body(it, first, last):
                for par in range(2):
                    g = 2 * it + par
                    end = last and par == 1
                    for step in range(NS):
                        take(g, par, end, SLOTS[step], SLOTS[step + 1])
                        if not end:
                            after(g, par, SLOTS[step + 1])
                        if step == 8 and not (first and par == 0):
                            invert(g - 1)

            for step in range(NS):
                take(-1, 1, False, SLOTS[step], SLOTS[step + 1], prologue=True)
                after(-1, 1, SLOTS[step + 1])
            run(dve, body)
            invert(z.G - 1)

        @block.tensor
        def _(pe):
            def fill(g, par, last, lo, hi, prologue=False):
                for k, bank, (ahead, item) in ring(g, last, lo, hi):
                    if prologue and item == "turn 1":
                        continue
                    gi, pi = g + ahead, (par + ahead) % 2
                    wait(pe, s_taken, k - 1)
                    if item in ("turn 0", "turn 1"):
                        qc = int(item[-1])
                        wait(pe, s_neg, 2 * (z.NC * gi + qc + 1), apart=True)
                        pe.transpose(pm[bank][0:MROWS, 0:P // 2].bitcast(BF16),
                                     neg[:, qc].rearrange("p s h t -> p (s h t)"), c["ident_b"][:, :]).then_inc(s_item, 1)
                        continue
                    qc, qt, kc, width, h0, n_heads = item
                    for j in range(n_heads):
                        to = pm[bank][:, j * width:(j + 1) * width]
                        diagonal = kc == qc
                        mm = pe.matmul(to, qs[pi][0:z.ROWS, qc, h0 + j, qt * P:(qt + 1) * P],
                                       ks[pi][0:z.ROWS, kc, h0 + j, 0:width],
                                       start=(j == 0), stop=not diagonal, skip_group_check=True)
                        if diagonal:
                            mm = pe.matmul(to[:, width - P:], c["ident_b"][:, :], c["causal"][:, :],
                                           start=False, stop=True, skip_group_check=True)
                    mm.then_inc(s_item, 2 if prologue and (k + 1) % NI == TURN[1] else 1)

            def scores(g, par, step, pair):
                n = NS * g + step
                qc, kb = STEPS[step]
                if kb == 0 and pair == 0:
                    wait(pe, s_rows[qc], 16 * (g + 1))
                wait(pe, s_exp, 2 * n + pair - 1)
                for h in (2 * pair, 2 * pair + 1):
                    mm = pe.matmul(st[pair][:, h % 2, 0:z.CT - q0(step)],
                                   ks[par][0:z.ROWS + MP, kb // z.TT, h, kb % z.TT * P:(kb % z.TT + 1) * P],
                                   qs[par][0:z.ROWS + MP, qc, h, q0(step):], start=True, stop=True)
                mm.then_inc(s_qk, 1)

            def weigh(g, par, step):
                n = NS * g + step
                qc, kb = STEPS[step]
                wait(pe, s_exp, 2 * n + 2)
                if step in MASKED:
                    wait(pe, s_mask, len(MASKED) * g + MASKED.index(step) + 1)
                if kb == 0:
                    wait(pe, s_raw, 2 * g - 1 + qc)
                    if qc == 0:
                        wait(pe, s_vg, g + 1)
                for h in range(HG):
                    mm = pe.matmul(po[qc][32 * h:32 * h + 32, q0(step):], vg[par][:, kb, h, :],
                                   probs[step % RING][:, h, 0:z.CT - q0(step)],
                                   start=(kb == 0), stop=(kb == z.TT * (qc + 1) - 1))
                mm.then_inc(s_pv, 1)

            def loaded(eng_it, ahead, tc):
                wait(pe, s_stack[ahead % 2][tc], 16 * LOADS * (eng_it + ahead // 2 + 1))

            def body(it, first, last):
                for par in range(2):
                    g = 2 * it + par
                    end = last and par == 1
                    for step in range(NS):
                        lo, hi = SLOTS[step], SLOTS[step + 1]
                        a, b, d = lo + (hi - lo + 3) // 4, lo + (hi - lo + 1) // 2, hi - (hi - lo) // 4
                        if step == 0 and not end:
                            loaded(it, par + 1, 0)
                        if step == z.TT and not end:
                            loaded(it, par + 1, 1)
                        scores(g, par, step, 0)
                        fill(g, par, end, lo, a)
                        scores(g, par, step, 1)
                        fill(g, par, end, a, d)
                        if step >= LAG:
                            weigh(g, par, step - LAG)
                        elif not (first and par == 0):
                            weigh(g - 1, 1 - par, NS - LAG + step)
                        fill(g, par, end, d, hi)

            pe.wait_ge(s_ones, 4)
            loaded(0, 0, 0)
            for step in range(NS):
                if step == z.TT:
                    loaded(0, 0, 1)
                fill(-1, 1, False, SLOTS[step], SLOTS[step + 1], prologue=True)
            run(pe, body)
            for step in range(NS - LAG, NS):
                weigh(z.G - 1, 1, step)



def ffn_phase(nc, z, c, x, residual, attn_t, out):
    TILES = z.S // P
    ER = EXPERTS * RANK // P
    NT = z.B * TILES
    with ExitStack() as ctx:
        def sb(name, shape, dt):
            return ctx.enter_context(nc.sbuf_tensor(name, shape, dt))

        def sem(name):
            return ctx.enter_context(nc.semaphore(name))

        def pair(name, shape):
            return sb(name + "_hi", shape, F32R), sb(name + "_lo", shape, F32R)

        res = residual[:, :, :, :, :].rearrange("p c g t f -> p (c g t f)").rearrange("p (n d) -> p n d", n=NT)
        xt = sb("x2_t", [P, z.B * z.DC, z.S], F32)
        wo_hi, wo_lo = pair("w_o", [P, z.DC, z.D])
        dn_hi, dn_lo = pair("down_t", [P, ER, z.D])
        up_hi, up_lo = pair("up_scaled", [P, ER, z.D])
        wf_hi, wf_lo = pair("w_ffn", [P, z.DC, z.D])
        a_hi, a_lo = pair("tile", [P, 2, z.DC, P])
        xn, ot = c["wo"][:, 0:2, :], c["wo"][:, 2:4, :]
        wsum = c["down"]
        stats = sb("stats2", [P, 2, 6], F32)
        mv = sb("mv2", [P, 2, 2], F32)
        small = sb("small2", [P, 2, 4], F32)
        mean = sb("mean", [P, z.B * z.DC], F32)
        gate_q = sb("gate_q", [KEY, z.B], F32)
        soft = sb("soft", [z.B, 4, EXPERTS], F32)
        spread = sb("spread", [z.B, z.B, EXPERTS], F32)
        ones = sb("ones", [z.B, P], F32)
        coeff = sb("coeff", [P, z.B, ER], F32)

        py = ctx.enter_context(nc.psum_tensor("py", [P, 2, z.D], F32))
        pt = ctx.enter_context(nc.psum_tensor("pt2", [P, 2, z.DC, P], F32))
        pw = ctx.enter_context(nc.psum_tensor("pw", [P, 2, z.D], F32))
        pg = ctx.enter_context(nc.psum_tensor("pg", [P, 2, z.D], F32))

        s_x = [sem(f"x_back{b}") for b in range(z.B)]
        s_hi = sem("w_hi_ready")
        s_lo = sem("w_lo_ready")
        s_dlo = sem("down_lo_ready")
        s_ahi = sem("tile_hi_ready")
        s_alo = sem("tile_lo_ready")
        s_y = sem("y_ready")
        s_res = sem("residual_ready")
        s_ln = sem("ln2_stats")
        s_root = sem("ln2_root")
        s_sqrt = sem("sqrt2_ready")
        s_xn = sem("xn2_ready")
        s_tr = sem("transposed2")
        s_xt = sem("xt_ready")
        s_mean = sem("mean_ready")
        s_gate = sem("gate_pe")
        s_gv = sem("gate_vector")
        s_ge = sem("gate_exp")
        s_uhi = sem("up_hi_ready")
        s_ulo = sem("up_lo_ready")
        s_eff = sem("w_ffn_summed_pe")
        s_sum = sem("w_ffn_with_base")
        s_whi = sem("w_ffn_hi_ready")
        s_wlo = sem("w_ffn_lo_ready")
        s_zp = sem("ffn_product_ready")
        s_o = sem("out_tile_ready")
        s_out = [sem(f"out_stored{n}") for n in range(2)]

        LN_STEPS, ROOT_STEPS = 3, 5
        block = ctx.enter_context(nc.Block())

        def pairs(eng, b, body, between=None):
            body(b, 0)
            if between:
                between()
            with eng.Fori(1, TILES // 2) as m:
                body(b, m)

        def attn_tile(b, t):
            return attn_t[:, b * z.DC:(b + 1) * z.DC, bass.ds(t * P, P)]

        def xt_tile(b, t):
            return xt[:, b * z.DC:(b + 1) * z.DC, bass.ds(t * P, P)]

        @block.sync
        def _(sp):
            for b in range(z.B):
                sp.dma_start(res[:, b * TILES:(b + 1) * TILES, :],
                             x[b].rearrange("(t p) d -> p t d", p=P)).then_inc(s_x[b], 16)
            dst = out.rearrange("b (t p) d -> (b t) p d", p=P)
            with sp.Fori(0, NT // 2) as n:
                for j in range(2):
                    sp.wait_ge(s_o, 2 * n + j + 1)
                    sp.dma_start(dst[bass.ds(2 * n + j, 1)].rearrange("a p d -> (a p) d"), ot[:, j, :]).then_inc(s_out[j], 16)
            for j in range(2):
                sp.wait_ge(s_out[j], NT // 2 * 16)

        @block.gpsimd
        def _(pool):
            pool.memset(ones[:, :], 1.0).then_inc(s_mean, 1)

            def lower(n, src, j):
                pool.wait_ge(s_ahi, n + 1)
                pool.tensor_tensor(a_lo[:, j], src, a_hi[:, j].bitcast(F32), ALU.subtract).then_inc(s_alo, 1)

            for b in range(z.B):
                with pool.Fori(0, TILES // 2) as m:
                    for j in range(2):
                        lower(b * TILES + 2 * m + j, attn_tile(b, 2 * m + j), j)
                if b == 0:
                    for k in range(ER):
                        pool.wait_ge(s_hi, z.DC + k + 1)
                        pool.tensor_tensor(dn_lo[:, k], c["down"][:, k], dn_hi[:, k].bitcast(F32),
                                           ALU.subtract).then_inc(s_dlo, 1)
            for b in range(z.B):
                with pool.Fori(0, TILES // 2) as m:
                    for j in range(2):
                        lower(NT + b * TILES + 2 * m + j, xt_tile(b, 2 * m + j), j)

        @block.scalar
        def _(act):
            for k in range(z.DC):
                act.copy(wo_hi[:, k], c["wo"][:, k]).then_inc(s_hi, 1)

            def first_tiles(b, m):
                for j in range(2):
                    n = b * TILES + 2 * m + j
                    wait(act, s_y, n - 1)
                    act.copy(a_hi[:, j], attn_tile(b, 2 * m + j)).then_inc(s_ahi, 1)
                for j in range(2):
                    n = b * TILES + 2 * m + j
                    wait(act, s_ln, LN_STEPS * n + 3)
                    act.activation(small[:, j, 1:2], small[:, j, 0:1], ACT.Sqrt).then_inc(s_sqrt, 1)
                for j in range(2):
                    n = b * TILES + 2 * m + j
                    wait(act, s_tr, n + 1)
                    act.copy(xt_tile(b, 2 * m + j), pt[:, j]).then_inc(s_xt, 1)

            pairs(act, 0, first_tiles)
            for k in range(ER):
                act.copy(dn_hi[:, k], c["down"][:, k]).then_inc(s_hi, 1)
            pairs(act, 1, first_tiles)

            def last_tiles(b, m):
                for j in range(2):
                    n = b * TILES + 2 * m + j
                    wait(act, s_zp, n - 1)
                    act.copy(a_hi[:, j], xt_tile(b, 2 * m + j)).then_inc(s_ahi, 1)

            act.wait_ge(s_y, NT)
            act.wait_ge(s_gv, 3)
            act.activation(soft[:, 1], soft[:, 0], ACT.Exp, bias=soft[:, 3, 0:1], scale=KEY ** -0.5,
                           accum_out=soft[:, 3, 1:2]).then_inc(s_ge, 1)
            for b in range(z.B):
                for k in range(z.DC):
                    n = b * z.DC + k
                    wait(act, s_sum, n + 1)
                    if k == 0 and b:
                        wait(act, s_zp, b * TILES)
                    act.copy(wf_hi[:, k], wsum[:, k]).then_inc(s_whi, 1)
                pairs(act, b, last_tiles)

        @block.vector
        def _(dve):
            for k in range(z.DC):
                wait(dve, s_hi, k + 1)
                dve.tensor_tensor(wo_lo[:, k], c["wo"][:, k], wo_hi[:, k].bitcast(F32), ALU.subtract).then_inc(s_lo, 1)

            def tile_ln(b, m, j):
                n = b * TILES + 2 * m + j
                base = LN_STEPS * n
                row = res[:, bass.ds(n, 1), :].rearrange("p a d -> p (a d)")
                wait(dve, s_y, n + 1)
                dve.tensor_tensor(row, py[:, j, :], row, ALU.add).then_inc(s_res, 1)
                wait(dve, s_res, n + 1, apart=True)
                dve.bn_stats(stats[:, j, :], row).then_inc(s_ln, 1)
                wait(dve, s_ln, base + 1, apart=True)
                dve.bn_aggr(mv[:, j, :], stats[:, j, :]).then_inc(s_ln, 1)
                wait(dve, s_ln, base + 2)
                dve.tensor_scalar(small[:, j, 0:1], mv[:, j, 1:2], EPS, None, ALU.add).then_inc(s_ln, 1)
                return row

            def tile_norm(b, m, j):
                n = b * TILES + 2 * m + j
                row = res[:, bass.ds(n, 1), :].rearrange("p a d -> p (a d)")
                part = [small[:, j, q:q + 1] for q in range(4)]
                rsqrt_newton(dve, part, s_root, ROOT_STEPS * n, s_sqrt, n + 1)
                wait(dve, s_tr, n - 1)
                dve.tensor_scalar(xn[:, j, :], row, mv[:, j, 0:1], part[3], ALU.subtract, ALU.mult).then_inc(s_xn, 1)

            def first_tiles(b, m):
                for j in range(2):
                    tile_ln(b, m, j)
                for j in range(2):
                    tile_norm(b, m, j)

            def mean_of(b):
                wait(dve, s_xt, TILES * (b + 1))
                dve.reduce_sum(mean[:, b * z.DC:(b + 1) * z.DC], xt[:, b * z.DC:(b + 1) * z.DC, :], AX.X).then_inc(s_mean, 1)

            dve.wait_ge(s_x[0], 16)
            pairs(dve, 0, first_tiles)
            dve.wait_ge(s_x[1], 16)
            pairs(dve, 1, first_tiles, between=lambda: mean_of(0))
            mean_of(1)
            dve.wait_ge(s_gate, 1)
            dve.tensor_scalar(gate_q[:, :], pg[:, 0, 0:z.B], 1.0 / z.S, None, ALU.mult).then_inc(s_gv, 1)
            dve.wait_ge(s_gate, 2)
            dve.tensor_copy(soft[:, 0], pg[0:z.B, 1, 0:EXPERTS])
            dve.reduce_max(soft[:, 2, 0:1], pg[0:z.B, 1, 0:EXPERTS], AX.X).then_inc(s_gv, 1)
            dve.wait_ge(s_gv, 2)
            dve.tensor_scalar(soft[:, 3, 0:1], soft[:, 2, 0:1], -KEY ** -0.5, None, ALU.mult).then_inc(s_gv, 1)
            dve.wait_ge(s_ge, 1)
            dve.reciprocal(soft[:, 3, 2:3], soft[:, 3, 1:2]).then_inc(s_gv, 1)
            dve.wait_ge(s_gv, 4)
            dve.tensor_scalar(soft[:, 2], soft[:, 1], soft[:, 3, 2:3], None, ALU.mult).then_inc(s_gv, 1)
            dve.wait_ge(s_gv, 5)
            for b in range(z.B):
                dve.tensor_scalar(spread[:, b], soft[:, 2], c["ident"][0:z.B, b:b + 1], None, ALU.mult).then_inc(s_gv, 1)
            dve.wait_ge(s_gate, 3)
            every = pg[:, 0, 0:z.B * EXPERTS].rearrange("p (b k r) -> p b k r", b=z.B, r=2)
            for half in range(2):
                rows = slice(RANK * half, RANK * (half + 1))
                dve.tensor_copy(coeff[rows, :, :], every[rows, :, :, half]).then_inc(s_gv, 1)
            dve.wait_ge(s_gv, 9)

            def scale_up(b):
                wait(dve, s_eff, b * z.DC)
                for k in range(ER):
                    dve.tensor_scalar(up_hi[:, k], c["up"][:, k], coeff[:, b, k:k + 1], None, ALU.mult).then_inc(s_uhi, 1)
                    wait(dve, s_uhi, b * ER + k + 1)
                    dve.scalar_tensor_tensor(out=up_lo[:, k], in0=c["up"][:, k], scalar=coeff[:, b, k:k + 1],
                                             in1=up_hi[:, k].bitcast(F32), op0=ALU.mult, op1=ALU.subtract).then_inc(s_ulo, 1)

            def effective(b):
                for k in range(z.DC):
                    n = b * z.DC + k
                    wait(dve, s_eff, n + 1)
                    dve.tensor_tensor(wsum[:, k], pw[:, k % 2, :], c["w_org"][:, k], ALU.add).then_inc(s_sum, 1)
                    wait(dve, s_whi, n + 1)
                    dve.tensor_tensor(wf_lo[:, k], wsum[:, k], wf_hi[:, k].bitcast(F32), ALU.subtract).then_inc(s_wlo, 1)

            def last_tiles(b, m):
                for j in range(2):
                    n = b * TILES + 2 * m + j
                    wait(dve, s_zp, n + 1)
                    wait(dve, s_out[j], (b * (TILES // 2) + m) * 16)
                    dve.tensor_tensor(ot[:, j, :], py[:, j, :], res[:, bass.ds(n, 1), :].rearrange("p a d -> p (a d)"),
                                      ALU.add).then_inc(s_o, 1)

            scale_up(0)
            effective(0)
            scale_up(1)
            pairs(dve, 0, last_tiles)
            effective(1)
            pairs(dve, 1, last_tiles)

        @block.tensor
        def _(pe):
            def first_tiles(b, m):
                for j in range(2):
                    n = b * TILES + 2 * m + j
                    wait(pe, s_alo, n + 1)
                    wait(pe, s_res, n - 1)
                    for k in range(z.DC):
                        mm = exact_product(pe, py[:, j, :], a_hi[:, j, k], a_lo[:, j, k], wo_hi[:, k], wo_lo[:, k],
                                           k == 0, k == z.DC - 1)
                    mm.then_inc(s_y, 1)
                for j in range(2):
                    n = b * TILES + 2 * m + j
                    wait(pe, s_xn, n + 1)
                    wait(pe, s_xt, n - 1)
                    for k in range(z.DC):
                        mm = pe.transpose(pt[:, j, k, :], xn[:, j, k * P:(k + 1) * P], c["ident"][:, :])
                    mm.then_inc(s_tr, 1)

            def last_tiles(b, m):
                for j in range(2):
                    n = b * TILES + 2 * m + j
                    wait(pe, s_alo, NT + n + 1)
                    wait(pe, s_o, n - 1)
                    for k in range(z.DC):
                        mm = exact_product(pe, py[:, j, :], a_hi[:, j, k], a_lo[:, j, k], wf_hi[:, k], wf_lo[:, k],
                                           k == 0, k == z.DC - 1)
                    mm.then_inc(s_zp, 1)

            pe.wait_ge(s_lo, z.DC)
            for b in range(z.B):
                pairs(pe, b, first_tiles)
            pe.wait_ge(s_mean, 1 + z.B)
            for k in range(z.DC):
                mm = pe.matmul(pg[:, 0, 0:z.B], c["wq"][:, k, :], mean[:, :].rearrange("p (b k) -> p k b", b=z.B)[:, k, :],
                               start=(k == 0), stop=(k == z.DC - 1))
            mm.then_inc(s_gate, 1)
            pe.wait_ge(s_gv, 1)
            pe.matmul(pg[0:z.B, 1, 0:EXPERTS], gate_q[:, :], c["keys"][:, :], start=True, stop=True).then_inc(s_gate, 1)
            pe.wait_ge(s_gv, 7)
            pe.matmul(pg[:, 0, 0:z.B * EXPERTS], ones[:, :], spread[:, :, :].rearrange("p b e -> p (b e)"),
                      start=True, stop=True).then_inc(s_gate, 1)
            for b in range(z.B):
                wait(pe, s_dlo, ER)
                for k in range(z.DC):
                    n = b * z.DC + k
                    wait(pe, s_sum, n - 1)
                    for r in range(ER):
                        if k == 0:
                            wait(pe, s_ulo, b * ER + r + 1)
                        cols = slice(k * P, (k + 1) * P)
                        mm = exact_product(pe, pw[:, k % 2, :], dn_hi[:, r, cols], dn_lo[:, r, cols],
                                           up_hi[:, r], up_lo[:, r], r == 0, r == ER - 1)
                    mm.then_inc(s_eff, 1)
                wait(pe, s_wlo, (b + 1) * z.DC)
                pairs(pe, b, last_tiles)



def _rotation_tables(z):
    import numpy as np
    inv = (1.0 / np.float32(THETA) ** (np.arange(0, z.HD, 2, dtype=np.float32) / np.float32(z.HD))).astype(np.float32)
    angle = np.arange(z.S, dtype=np.float32)[:, None] * inv[None, :]
    both = np.stack([np.cos(angle), np.sin(angle)]).astype(np.float32)
    rows = np.tile(np.repeat(both.transpose(2, 0, 1), z.GH, axis=0), (4, 1, 1))
    chunks = rows.reshape(P, 2, z.NC, z.CT).transpose(2, 0, 1, 3)
    return np.ascontiguousarray(np.repeat(chunks, z.B, axis=0))


def kernel(L0_attn_hidden_states, L0_attn_wq, L0_attn_wk, L0_attn_wv, L0_attn_wo, L0_ffn_W_org,
           L0_ffn_lora_down, L0_ffn_lora_up, L0_ffn_lora_keys, L0_ffn_Wq):
    import numpy as np
    import concourse.bacc as bacc
    from concourse.bass_utils import run_bass_kernel_spmd

    x = np.asarray(L0_attn_hidden_states)
    z = Sizes(*x.shape)

    def by_half(w):
        w = np.asarray(w).reshape(z.D, z.SG, 4, z.GH, 2, z.HALF)
        return w.transpose(0, 1, 4, 2, 5, 3).reshape(z.D, z.D)

    arrays = {
        "x": x,
        "xc": x.reshape(z.B, z.NC, z.CT, z.D).transpose(1, 0, 2, 3).reshape(z.CHUNKS, z.CT, z.D),
        "w_in": np.concatenate([by_half(L0_attn_wq), by_half(L0_attn_wk), np.asarray(L0_attn_wv)], axis=1),
        "rope": _rotation_tables(z),
        "w_o": np.asarray(L0_attn_wo),
        "w_org_t": np.asarray(L0_ffn_W_org).T,
        "down_t": np.asarray(L0_ffn_lora_down).transpose(0, 2, 1).reshape(EXPERTS * RANK, z.D),
        "up": np.asarray(L0_ffn_lora_up).reshape(EXPERTS * RANK, z.D),
        "keys_t": np.asarray(L0_ffn_lora_keys).T,
        "wq_t": np.asarray(L0_ffn_Wq).T,
    }
    arrays = {n: np.ascontiguousarray(a) for n, a in arrays.items()}
    nc = bacc.Bacc("TRN2", target_bir_lowering=False, num_devices=1)
    args = [nc.dram_tensor("in_" + n, a.shape, mybir.dt.from_np(a.dtype), kind="ExternalInput").ap() for n, a in arrays.items()]
    args.append(nc.dram_tensor("y", x.shape, F32, kind="ExternalOutput").ap())
    layer_kernel(nc, *args)
    result = run_bass_kernel_spmd(nc, [{"in_" + n: a for n, a in arrays.items()}], core_ids=[0])
    return result.results[0]["y"]
```

```python
from contextlib import ExitStack

import concourse.bass as bass
from concourse import mybir

ALU = mybir.AluOpType
ACT = mybir.ActivationFunctionType
AX = mybir.AxisListType
F32 = mybir.dt.float32
F32R = mybir.dt.float32r
BF16 = mybir.dt.bfloat16

P = 128
HEADS = 32
THETA = 10000.0
EPS = 1e-5
EXPERTS, RANK, KEY = 8, 64, 128


def wait(eng, sem, value, apart=False):
    if isinstance(value, int):
        if value > 0:
            eng.wait_ge(sem, value)
        return
    eng.wait_ge(sem, value)
    if apart:
        eng.nop(nofuse=True)


class Sizes:

    def __init__(s, batches, seq, dim):
        s.B, s.S, s.D = batches, seq, dim
        s.HD = dim // HEADS
        s.HALF = s.HD // 2
        s.DC = dim // P
        s.CT = 512
        s.NC = seq // s.CT
        s.TT = s.CT // P
        s.CHUNKS = batches * s.NC
        s.SG = HEADS // 16
        s.GH = 4
        s.GB = HEADS // s.GH
        s.G = batches * s.GB
        s.KT = seq // P
        s.ROWS = 6 * s.HD


Q_RUNS = [(0, 3), (0, 2), (0, 1)]
K_PARTS = [(0, 3), (1, 2), (2, 1)]


def layer_kernel(nc, x, xc, w_in, rope, w_o, w_org_t, down_t, up, keys_t, wq_t, out):
    z = Sizes(*x.shape)
    scratch = {n: nc.dram_tensor(f"{n}_parts", [z.NC * z.G, 3, 2, z.HALF, z.GH, z.CT], BF16,
                                 kind="Internal").ap() for n in "qk"}
    with ExitStack() as keep:
        def sb(name, shape, dt):
            return keep.enter_context(nc.sbuf_tensor(name, shape, dt))

        def sem(name):
            return keep.enter_context(nc.semaphore(name))

        c = {
            "ident": sb("ident", [P, P], F32),
            "ident_b": sb("ident_b", [P, P], BF16),
            "causal": sb("causal", [P, P], BF16),
            "wo": sb("wo", [P, z.DC, z.D], F32),
            "w_org": sb("w_org", [P, z.DC, z.D], F32),
            "down": sb("down", [P, z.DC, z.D], F32),
            "up": sb("up", [P, z.DC, z.D], F32),
            "s_weights": sem("weights_loaded"),
            "s_put": [sem("parts_stored_even"), sem("parts_stored_odd")],
            "s_const": sem("constants_ready"),
        }
        values = sb("values", [P, z.NC, z.G, z.TT, z.GH * z.HD], F32)
        project_phase(nc, z, c, xc, w_in, rope, (w_o, w_org_t, down_t, up), scratch, values)
        attn_t = sb("attn_t", [P, z.DC, z.B * z.S], F32)
        for name in ("wo", "down"):
            for half in ("hi", "lo"):
                c[f"{name}_{half}"] = sb(f"{name}_{half}", [P, z.DC, z.D], F32R)
        c["s_residual"] = sem("residual_loaded")
        finish = Finish(nc, z, sb, sem, attn_t)
        attention_phase(nc, z, c, x, scratch, values, finish)
        ffn_phase(nc, z, c, values, attn_t, finish, keys_t, wq_t, out)


def residual_view(z, values):
    return values[:, :, :, :, :].rearrange("p c g t f -> p (c g t f)").rearrange("p (n d) -> p n d", n=z.B * z.KT)


class Finish:

    def __init__(s, nc, z, sb, sem, attn_t):
        s.z, s.attn_t = z, attn_t
        s.raw = sb("out_raw", [P, z.NC, z.CT], F32)
        s.sums = sb("sums", [P, z.GH * z.S // P], F32)
        s.num = sb("numerator", [P, z.S], F32)
        s.inv = sb("inverse_sums", [P, z.S], F32)
        s.s_raw = sem("out_raw_ready")
        s.s_bounce = sem("out_in_dram")
        s.s_num = sem("numerator_loaded")
        s.s_sums = sem("sums_loaded")
        s.s_inv = sem("reciprocal_ready")
        s.s_back = sem("reciprocal_in_dram")
        s.s_spread = sem("reciprocal_spread")
        s.s_free = sem("numerator_free")
        s.bounce = nc.dram_tensor("out_by_group", [z.G, z.GH, 2 * z.HD, z.S], F32, kind="Internal").ap()
        s.inverse = nc.dram_tensor("inverse_by_group", [z.G, z.GH, z.S], F32, kind="Internal").ap()

    def rows_out(s, sp, g):
        sp.wait_ge(s.s_raw, 2 * (g + 1))
        sp.nop(nofuse=True)
        sp.dma_start(s.bounce[bass.ds(g, 1)].rearrange("a h r t -> (a h r) t"),
                     s.raw[:, :, :].rearrange("p c t -> p (c t)")).then_inc(s.s_bounce, 16)

    def rows_in(s, sp, g, par, it):
        z = s.z
        sp.wait_ge(s.s_bounce, 16 * (g + 1))
        sp.nop(nofuse=True)
        wait(sp, s.s_back, 16 * g, apart=True)
        one = s.bounce[bass.ds(g, 1)].rearrange("a h r t -> (a h) r t")
        sp.dma_start(s.sums[:, :], one[:, z.HD, :].rearrange("h (x y) -> h x y", x=P // z.GH)).then_inc(s.s_sums, 16)
        sp.wait_ge(s.s_free, it + 1)
        sp.nop(nofuse=True)
        sp.dma_start(s.num[64 * par:64 * par + 64, :], one[:, 0:z.HD, :]).then_inc(s.s_num, 16)

    def inverse_out(s, sp, g):
        sp.wait_ge(s.s_inv, g + 1)
        sp.nop(nofuse=True)
        sp.dma_start(s.inverse[bass.ds(g, 1)].rearrange("a h (x y) -> (a h x) y", x=P // s.z.GH),
                     s.sums[:, :]).then_inc(s.s_back, 16)

    def inverse_in(s, sp, g, par):
        z = s.z
        sp.wait_ge(s.s_back, 16 * (g + 1))
        sp.nop(nofuse=True)
        one = s.inverse[bass.ds(g, 1)].rearrange("a h t -> h a t").broadcast_to([z.GH, z.HD, z.S])
        sp.dma_start(s.inv[64 * par:64 * par + 64, :], one).then_inc(s.s_spread, 16)

    def invert(s, dve, g):
        dve.wait_ge(s.s_sums, 16 * (g + 1))
        dve.reciprocal(s.sums[:, :], s.sums[:, :]).then_inc(s.s_inv, 1)

    def divide(s, eng, it, b, k):
        eng.wait_ge(s.s_num, 32 * (it + 1))
        eng.wait_ge(s.s_spread, 32 * (it + 1))
        eng.tensor_tensor(s.attn_t[:, bass.ds(k, 1), b * s.z.S:(b + 1) * s.z.S].rearrange("p a t -> p (a t)"),
                           s.num[:, :], s.inv[:, :], ALU.mult).then_inc(s.s_free, 1)



def project_phase(nc, z, c, xc, w_in, rope, weights, scratch, values):
    NU = 2 * z.SG
    QKC = 2 * z.D
    with ExitStack() as ctx:
        def sb(name, shape, dt):
            return ctx.enter_context(nc.sbuf_tensor(name, shape, dt))

        def sem(name):
            return ctx.enter_context(nc.semaphore(name))

        parts = sb("parts", [P, 2, 3, 2, z.CT], BF16)
        wraw = [c[name][:, :, :].rearrange("p a n -> p (a n)")[:, 0:3 * z.D] for name in ("wo", "w_org", "down", "up")]
        whi = sb("whi", [P, z.DC, 3 * z.D], F32R)
        wlo = sb("wlo", [P, z.DC, 3 * z.D], F32R)
        xin = sb("xin", [P, z.TT, z.D], F32)
        xn = sb("xn", [P, z.TT, z.D], F32)
        xhi = sb("xhi", [P, 2, z.DC, z.CT], F32R)
        xlo = sb("xlo", [P, 2, z.DC, z.CT], F32R)
        table = sb("table", [P, 2, z.CT], F32)
        prod = sb("prod", [P, 2, 4, z.CT], F32)
        rot = sb("rot", [P, 2, 2, z.CT], F32)
        rest = sb("rest", [P, 2, z.CT], F32)
        stats = sb("stats", [P, z.TT, 6], F32)
        mv = sb("mv", [P, z.TT, 2], F32)
        small = sb("small", [P, 4, z.TT], F32)

        pt = ctx.enter_context(nc.psum_tensor("pt", [P, 2, z.DC, P], F32))
        pu = ctx.enter_context(nc.psum_tensor("pu", [P, 2, 2, z.CT], F32))
        pv = ctx.enter_context(nc.psum_tensor("pv", [P, 2, z.D], F32))

        s_wraw = [sem(f"wraw_loaded{n}") for n in range(3)]
        s_whi = sem("whi_ready")
        s_wlo = [sem(f"wlo_ready{n}") for n in range(3)]
        s_x = [sem(f"x_loaded{t}") for t in range(z.TT)]
        s_table = sem("table_loaded")
        s_ln = sem("ln_small")
        s_sqrt = sem("sqrt_ready")
        s_xn = sem("xn_ready")
        s_tr = sem("transposed")
        s_xhi = sem("xhi_ready")
        s_xlo = sem("xlo_ready")
        s_unit = sem("unit_projected")
        s_v = sem("v_projected")
        s_vout = sem("v_stored")
        s_prod = sem("products_ready")
        s_rot = sem("rotated")
        s_p1 = sem("part1_ready")
        s_rest = sem("rest_ready")
        s_p2 = sem("part2_ready")
        s_p3 = sem("part3_ready")
        s_put = c["s_put"]
        s_setup = sem("pool_setup")

        LN_STEPS = 6 + 2
        SECTIONS = [slice(n * z.D, (n + 1) * z.D) for n in range(3)]
        block = ctx.enter_context(nc.Block())

        @block.sync
        def _(sp):
            def load_x(i):
                wait(sp, s_xn, z.TT * i)
                for t in range(z.TT):
                    src = xc[bass.ds(i, 1), t * P:(t + 1) * P, :].rearrange("a p d -> (a p) d")
                    sp.dma_start(xin[:, t, :], src).then_inc(s_x[t], 16)

            def load_table(i):
                wait(sp, s_prod, NU * 2 * i)
                sp.dma_start(table[:, :, :], rope[bass.ds(i, 1)].rearrange("a p s t -> p (a s) t")).then_inc(s_table, 16)

            def store_parts(i, u):
                n = NU * i + u
                to = scratch["qk"[u // z.SG]]
                g = u % z.SG
                for part, ready in enumerate((s_p1, s_p2, s_p3)):
                    sp.wait_ge(ready, n + 1)
                    sp.nop(nofuse=True)
                    for half in range(2):
                        dst = to[bass.ds(i * z.GB + g * z.GH, z.GH), part, half].rearrange("g e h t -> g (e h) t")
                        sp.dma_start(dst, parts[:, u % 2, part, half, :]).then_inc(s_put[u % 2], 16)

            def body(i, left):
                for u in range(NU):
                    if u == NU - 1 and left >= 1:
                        load_table(i + 1)
                    store_parts(i, u)
                    if u == 1 and left >= 2:
                        load_x(i + 2)

            load_x(0)
            for n, cols in enumerate(SECTIONS):
                for k in range(z.DC):
                    sp.dma_start(wraw[k][:, cols], w_in[k * P:(k + 1) * P, cols]).then_inc(s_wraw[n], 16)
            load_table(0)
            load_x(1)
            with sp.Fori(0, z.CHUNKS - 2) as i:
                body(i, 2)
            body(z.CHUNKS - 2, 1)
            w_o, w_org_t, down_t, up = weights
            for n in range(3):
                sp.wait_ge(s_wlo[n], z.DC)
            for name, src in (("wo", w_o), ("w_org", w_org_t), ("down", down_t), ("up", up)):
                sp.dma_start(c[name][:, :, :], src.rearrange("(a p) n -> p a n", p=P)).then_inc(c["s_weights"], 16)
            body(z.CHUNKS - 1, 0)
            sp.wait_ge(c["s_weights"], 4 * 16)

        def split_rest(eng, n, k):
            cols = SECTIONS[n]
            eng.wait_ge(s_whi, n * z.DC + k + 1)
            eng.tensor_tensor(wlo[:, k, cols], wraw[k][:, cols], whi[:, k, cols].bitcast(F32), ALU.subtract).then_inc(s_wlo[n], 1)

        def x_tile(buf, slot, t):
            return buf[:, bass.ds(slot, 1), :, t * P:(t + 1) * P].rearrange("p a k t -> p (a k) t")

        @block.gpsimd
        def _(pool):
            pool.memset(c["ident"][:, :], 0.0).then_inc(s_setup, 1)
            pool.memset(c["ident_b"][:, :], 0.0).then_inc(s_setup, 1)
            pool.memset(c["causal"][:, :], 0.0).then_inc(s_setup, 1)
            pool.wait_ge(s_setup, 3)
            for m in (c["ident"], c["ident_b"]):
                pool.affine_select(out=m[:, :], in_=m[:, :], compare_op=ALU.not_equal, fill=1.0, base=0,
                                   pattern=[[-1, P]], channel_multiplier=1).then_inc(c["s_const"], 1)
            pool.affine_select(out=c["causal"][:, :], in_=c["causal"][:, :], compare_op=ALU.is_ge, fill=-3e38,
                               base=0, pattern=[[-1, P]], channel_multiplier=1).then_inc(c["s_const"], 1)

            def rotate(i):
                for u in range(NU):
                    n = NU * i + u
                    pr, ro = prod[:, u % 2], rot[:, u % 2]
                    wait(pool, s_rest, n - 1)
                    pool.wait_ge(s_prod, 2 * n + 1)
                    pool.tensor_tensor(ro[:, 0], pr[:, 0], pr[:, 1], ALU.subtract).then_inc(s_rot, 1)
                    pool.wait_ge(s_prod, 2 * n + 2)
                    pool.tensor_tensor(ro[:, 1], pr[:, 2], pr[:, 3], ALU.add).then_inc(s_rot, 1)

            for n in range(2):
                for k in range(z.DC):
                    split_rest(pool, n, k)
            rotate(0)
            with pool.Fori(1, z.CHUNKS) as i:
                rotate(i)

        @block.scalar
        def _(act):
            def root(i):
                act.wait_ge(s_ln, LN_STEPS * i + 3)
                act.activation(small[:, 1], small[:, 0], ACT.Sqrt).then_inc(s_sqrt, 1)

            def upper(i, slot, t):
                act.wait_ge(s_tr, z.TT * i + t + 1)
                act.copy(x_tile(xhi, slot, t), pt[:, t % 2]).then_inc(s_xhi, 1)

            def part1(i, u):
                n = NU * i + u
                wait(act, s_put[u % 2], (i * (NU // 2) + u // 2) * 96)
                act.wait_ge(s_rot, 2 * n + 2)
                act.copy(parts[:, u % 2, 0], rot[:, u % 2]).then_inc(s_p1, 1)

            def part2(i, u):
                act.wait_ge(s_rest, NU * i + u + 1)
                act.copy(parts[:, u % 2, 1], rest[:, :, :]).then_inc(s_p2, 1)

            def store_v(i, t):
                act.wait_ge(s_v, z.TT * i + t + 1)
                act.copy(values[:, :, :, :, :].rearrange("p n g t f -> p (n g) t f")[:, bass.ds(i * z.GB, z.GB), t, :],
                         pv[:, t % 2].rearrange("p (g f) -> p g f", g=z.GB)).then_inc(s_vout, 1)

            def whole_hi(n):
                act.wait_ge(s_wraw[n], 16 * z.DC)
                for k in range(z.DC):
                    act.copy(whi[:, k, SECTIONS[n]], wraw[k][:, SECTIONS[n]]).then_inc(s_whi, 1)

            def body(i, slot, last=False):
                if not last:
                    root(i + 1)
                for u in range(NU - 2):
                    part1(i, u)
                    part2(i, u)
                part1(i, NU - 2)
                if not last:
                    upper(i + 1, slot, 0)
                    upper(i + 1, slot, 1)
                part2(i, NU - 2)
                store_v(i, 0)
                if not last:
                    upper(i + 1, slot, 2)
                    upper(i + 1, slot, 3)
                part1(i, NU - 1)
                store_v(i, 1)
                part2(i, NU - 1)
                for t in range(2, z.TT):
                    store_v(i, t)

            root(0)
            whole_hi(0)
            for t in range(z.TT):
                upper(0, 0, t)
            whole_hi(1)
            whole_hi(2)
            body(0, 1)
            with act.Fori(1, z.CHUNKS - 1) as i:
                body(i, i - 1)
            body(z.CHUNKS - 1, None, last=True)

        @block.vector
        def _(dve):
            def ln_stats(i):
                base = LN_STEPS * i
                for t in range(z.TT):
                    dve.wait_ge(s_x[t], 16 * (i + 1))
                    dve.nop(nofuse=True)
                    ins = dve.bn_stats(stats[:, t, :], xin[:, t, :])
                ins.then_inc(s_ln, 1)
                dve.wait_ge(s_ln, base + 1)
                dve.nop(nofuse=True)
                for t in range(z.TT):
                    ins = dve.bn_aggr(mv[:, t, :], stats[:, t, :])
                ins.then_inc(s_ln, 1)
                dve.wait_ge(s_ln, base + 2)
                dve.tensor_scalar(small[:, 0], mv[:, :, 1], EPS, None, ALU.add).then_inc(s_ln, 1)

            def ln_apply(i):
                rsqrt_newton(dve, [small[:, n] for n in range(4)], s_ln, LN_STEPS * i + 3, s_sqrt, i + 1)
                wait(dve, s_tr, z.TT * i)
                for t in range(z.TT):
                    dve.tensor_scalar(xn[:, t, :], xin[:, t, :], mv[:, t, 0:1], small[:, 3, t:t + 1],
                                      ALU.subtract, ALU.mult).then_inc(s_xn, 1)

            def lower(i, slot, t):
                dve.wait_ge(s_xhi, z.TT * i + t + 1)
                dve.tensor_tensor(x_tile(xlo, slot, t), pt[:, t % 2], x_tile(xhi, slot, t).bitcast(F32),
                                  ALU.subtract).then_inc(s_xlo, 1)

            def products(i, u, half):
                n = NU * i + u
                a, b = pu[:, u % 2, 0, :], pu[:, u % 2, 1, :]
                if half == 0:
                    dve.wait_ge(s_unit, n + 1)
                    wait(dve, s_rot, 2 * n - 2)
                    dve.tensor_tensor(prod[:, u % 2, 0], a, table[:, 0], ALU.mult)
                    dve.tensor_tensor(prod[:, u % 2, 1], b, table[:, 1], ALU.mult).then_inc(s_prod, 1)
                else:
                    dve.tensor_tensor(prod[:, u % 2, 2], b, table[:, 0], ALU.mult)
                    dve.tensor_tensor(prod[:, u % 2, 3], a, table[:, 1], ALU.mult).then_inc(s_prod, 1)

            def rest_of(i, u):
                n = NU * i + u
                wait(dve, s_p3, n)
                dve.wait_ge(s_p1, n + 1)
                dve.tensor_tensor(rest[:, :, :], rot[:, u % 2], parts[:, u % 2, 0], ALU.subtract).then_inc(s_rest, 1)

            def part3(i, u):
                n = NU * i + u
                dve.wait_ge(s_p2, n + 1)
                dve.tensor_tensor(parts[:, u % 2, 2], rest[:, :, :], parts[:, u % 2, 1], ALU.subtract).then_inc(s_p3, 1)

            def units(i, slot, last=False):
                if not last:
                    ln_stats(i + 1)
                    ln_apply(i + 1)
                dve.wait_ge(s_table, 16 * (i + 1))
                for u in range(NU - 1):
                    products(i, u, 0)
                    if u:
                        rest_of(i, u - 1)
                    products(i, u, 1)
                    if u:
                        part3(i, u - 1)
                products(i, NU - 1, 0)
                rest_of(i, NU - 2)
                if not last:
                    lower(i + 1, slot, 0)
                    lower(i + 1, slot, 1)
                products(i, NU - 1, 1)
                part3(i, NU - 2)
                if not last:
                    lower(i + 1, slot, 2)
                    lower(i + 1, slot, 3)
                rest_of(i, NU - 1)
                part3(i, NU - 1)

            ln_stats(0)
            ln_apply(0)
            for t in range(z.TT):
                lower(0, 0, t)
            for k in range(z.DC):
                split_rest(dve, 2, k)
            units(0, 1)
            with dve.Fori(1, z.CHUNKS - 1) as i:
                units(i, i - 1)
            units(z.CHUNKS - 1, None, last=True)

        @block.tensor
        def _(pe):
            pe.wait_ge(c["s_const"], 3)

            def transpose(i, t):
                pe.wait_ge(s_xn, z.TT * i + t + 1)
                wait(pe, s_xlo, z.TT * i + t - 1)
                for k in range(z.DC):
                    mm = pe.transpose(pt[:, t % 2, k, :], xn[:, t, k * P:(k + 1) * P], c["ident"][:, :])
                mm.then_inc(s_tr, 1)

            def units(i, slot, first=False):
                pe.wait_ge(s_xlo, z.TT * (i + 1))
                hi, lo = (buf[:, bass.ds(slot, 1)].rearrange("p a k t -> p (a k) t") for buf in (xhi, xlo))
                for u in range(NU):
                    n = NU * i + u
                    wait(pe, s_prod, 2 * n - 2)
                    for half in range(2):
                        col = slice(u * 256 + half * P, u * 256 + (half + 1) * P)
                        for k in range(z.DC):
                            if first and half == 0 and u % z.SG == 0:
                                pe.wait_ge(s_wlo[u // z.SG], k + 1)
                            mm = exact_product(pe, pu[:, u % 2, half, :], whi[:, k, col], wlo[:, k, col],
                                               hi[:, k], lo[:, k], k == 0, k == z.DC - 1)
                    mm.then_inc(s_unit, 1)

            def project_v(i, slot, t, first=False):
                wait(pe, s_vout, z.TT * i + t - 1)
                for k in range(z.DC):
                    if first and t == 0:
                        pe.wait_ge(s_wlo[2], k + 1)
                    mm = exact_product(pe, pv[:, t % 2, :], x_tile(xhi, slot, t)[:, k], x_tile(xlo, slot, t)[:, k],
                                       whi[:, k, QKC:], wlo[:, k, QKC:], k == 0, k == z.DC - 1)
                mm.then_inc(s_v, 1)

            def body(i, slot, first=False, last=False):
                units(i, slot, first)
                for t in range(z.TT):
                    if not last and t < 2:
                        transpose(i + 1, 2 * t)
                        transpose(i + 1, 2 * t + 1)
                    project_v(i, slot, t, first)

            for t in range(z.TT):
                transpose(0, t)
            for i in range(z.CHUNKS):
                body(i, i % 2, first=(i == 0), last=(i == z.CHUNKS - 1))


def exact_product(pe, out, a_hi, a_lo, b_hi, b_lo, first, last):
    pe.matmul(out, a_hi, b_hi, start=first, stop=False)
    pe.matmul(out, a_hi, b_lo, start=False, stop=False)
    return pe.matmul(out, a_lo, b_hi, start=False, stop=last)


def rsqrt_newton(dve, small, s_step, base, s_sqrt, roots):
    v, s0, t, r = small
    dve.wait_ge(s_sqrt, roots)
    dve.reciprocal(t, s0).then_inc(s_step, 1)
    dve.wait_ge(s_step, base + 1)
    dve.tensor_tensor(t, t, v, ALU.mult).then_inc(s_step, 1)
    dve.wait_ge(s_step, base + 2)
    dve.tensor_tensor(t, t, s0, ALU.add).then_inc(s_step, 1)
    dve.wait_ge(s_step, base + 3)
    dve.reciprocal(r, t).then_inc(s_step, 1)
    dve.wait_ge(s_step, base + 4)
    dve.tensor_scalar(r, r, 2.0, None, ALU.mult).then_inc(s_step, 1)
    dve.wait_ge(s_step, base + 5)



def attention_phase(nc, z, c, x, scratch, values, finish):
    STEPS = [(qc, kb) for qc in range(z.NC) for kb in range(z.TT * (qc + 1))]
    NS = len(STEPS)
    RING = 3
    LAG = 2
    QT, HG = z.TT, z.GH
    MP = 2
    MROWS = MP * HG * QT

    tiles = []
    for qc in range(z.NC):
        for qt in range(QT):
            for kc in range(qc + 1):
                width = z.CT if kc < qc else (qt + 1) * P
                n = z.CT // width
                tiles.append([(qc, qt, kc, width, h, min(n, HG - h)) for h in range(0, HG, n)])
    chunk_tiles = [sum(tiles[:QT], []), sum(tiles[QT:], [])]
    T0, AFTER = len(chunk_tiles[0]), 4
    ITEMS = [(1, t) for t in chunk_tiles[0]]
    ITEMS.insert(4, (0, "turn 1"))
    ITEMS += [(1, t) for t in chunk_tiles[1][:AFTER]] + [(1, "turn 0")] + [(1, t) for t in chunk_tiles[1][AFTER:]]
    NI = len(ITEMS)
    TURN = {1: 4, 0: T0 + 1 + AFTER}
    SLOTS = [0, 4, 7, 10, 12, 17, 21, 25, 29, 33, 36, 38, NI]
    assert NI % 3 == 1 and ITEMS[TURN[0]][1] == "turn 0"
    BANK = [n % 3 for n in range(NI - 1)] + [1]
    MASKED = [s for s, (qc, kb) in enumerate(STEPS) if kb >= z.TT * qc]

    def q0(step):
        qc, kb = STEPS[step]
        return max(0, kb - z.TT * qc) * P

    with ExitStack() as ctx:
        def sb(name, shape, dt):
            return ctx.enter_context(nc.sbuf_tensor(name, shape, dt))

        def sem(name):
            return ctx.enter_context(nc.semaphore(name))

        qs = [sb(f"q_stack{n}", [P, z.NC, HG, z.CT], BF16) for n in range(2)]
        ks = [sb(f"k_stack{n}", [P, z.NC, HG, z.CT], BF16) for n in range(2)]
        probs = [sb(f"probs{n}", [P, HG, z.CT], F32) for n in range(RING)]
        vg = [sb(f"v_group{n}", [P, z.KT, HG, 2 * z.HD], F32) for n in range(2)]
        top = sb("row_max", [P, 2, z.NC, HG, QT], F32)
        top2 = sb("row_max_late", [P, 2, HG, QT], F32)
        neg = sb("neg_parts", [P, z.NC, MP, HG, QT], BF16)
        rows = [sb(f"neg_rows{n}", [MROWS, P], BF16) for n in range(z.NC)]

        st = [ctx.enter_context(nc.psum_tensor(f"scores_t{n}", [P, 2, z.CT], F32)) for n in range(2)]
        po = ctx.enter_context(nc.psum_tensor("out_t", [P, z.CT], F32))
        pm = [ctx.enter_context(nc.psum_tensor(f"max_bank{n}", [P, z.CT], F32)) for n in range(3)]

        s_ones = sem("stack_ones_ready")
        s_vones = sem("v_ones_ready")
        s_stack = [[sem(f"stack_loaded{n}_{qc}") for qc in range(z.NC)] for n in range(2)]
        s_item = sem("max_bank_filled")
        s_taken = sem("max_bank_read")
        s_comb = sem("max_combined")
        s_neg = sem("neg_steps")
        s_rows = [sem(f"neg_rows_loaded{n}") for n in range(z.NC)]
        s_qk = sem("scores_ready")
        s_exp = sem("exp_done")
        s_mask = sem("masked")
        s_pv = sem("pv_done")
        s_vg = sem("v_group_ready")
        s_hi = sem("w_hi_ready")
        s_lo = sem("w_lo_ready")

        ITERS = z.G // 2
        LOADS = len(Q_RUNS) + len(K_PARTS)

        split = [(c[n], c[n + "_hi"], c[n + "_lo"]) for n in ("wo", "down")]

        block = ctx.enter_context(nc.Block())

        def turned(g, qc, last):
            if last:
                return NI * (g + 1) + 1
            return NI * (g + 1 - (1 - qc)) + TURN[qc] + 1

        def ring(g, last, lo, hi):
            if last:
                return [(NI * (g + 1), 0, (0, "turn 1"))] if lo <= TURN[1] < hi else []
            return [(NI * (g + 1) + n, n, (ITEMS[n][0], ITEMS[n][1])) for n in range(lo, hi)]

        def emptied(k, n):
            return k - 1 if n in (1, NI - 1) else k - 2

        def run(eng, body):
            body(0, True, False)
            with eng.Fori(1, ITERS - 1) as it:
                body(it, False, False)
            body(ITERS - 1, False, True)

        @block.sync
        def _(sp):
            def load_stacks(g, par, tc):
                last_reader = NS - 1 if tc else NS - 1 - z.TT
                wait(sp, s_qk, 2 * (NS * (g - 2) + last_reader + 1), apart=True)
                own_q, own_k = (scratch[n][bass.ds(g + tc * z.G, 1)].rearrange("g s f e h t -> (g s f e) (h t)")
                                for n in "qk")
                row = 0
                for part, n in Q_RUNS:
                    sp.dma_start(qs[par][row:row + z.HD * n, tc].rearrange("p h t -> p (h t)"),
                                 own_q[z.HD * part:z.HD * (part + n)]).then_inc(s_stack[par][tc], 16)
                    row += z.HD * n
                row = 0
                for part, times in K_PARTS:
                    src = own_k[z.HD * part:z.HD * (part + 1)].rearrange("(a p) t -> a p t", a=1)
                    sp.dma_start(ks[par][row:row + z.HD * times, tc].rearrange("p h t -> p (h t)"),
                                 src.broadcast_to([times, z.HD, HG * z.CT])).then_inc(s_stack[par][tc], 16)
                    row += z.HD * times

            def load_residual():
                sp.wait_ge(s_vg, z.G)
                for b in range(z.B):
                    sp.dma_start(residual_view(z, values)[:, b * z.KT:(b + 1) * z.KT, :],
                                 x[b].rearrange("(t p) d -> p t d", p=P)).then_inc(c["s_residual"], 16)

            def body(it, first, last):
                for par in range(2):
                    g = 2 * it + par
                    before = not (first and par == 0)
                    if not (last and par == 1):
                        load_stacks(g + 1, 1 - par, 1)
                    if before:
                        finish.rows_out(sp, g - 1)
                        finish.rows_in(sp, g - 1, 1 - par, it if par else it - 1)
                    if not last:
                        load_stacks(g + 2, par, 0)
                    if last and par == 1:
                        load_residual()
                    if before:
                        finish.inverse_out(sp, g - 1)
                        finish.inverse_in(sp, g - 1, 1 - par)

            PUT = z.SG * 6 * 16
            for qc in range(z.NC):
                for n in range(2):
                    sp.wait_ge(c["s_put"][n], PUT * (z.B * qc + 1))
                load_stacks(0, 0, qc)
            load_stacks(1, 1, 0)
            for n in range(2):
                sp.wait_ge(c["s_put"][n], PUT * z.CHUNKS)
            run(sp, body)
        @block.gpsimd
        def _(pool):
            for n in range(2):
                pool.memset(vg[n][:, :, :, z.HD:], 1.0).then_inc(s_vones, 1)
            pool.wait_ge(s_vones, 2)
            pool.memset(ks[1][z.ROWS:, :, :, :], 1.0).then_inc(s_ones, 1)
            pool.wait_ge(s_ones, 2)

            def copy_v(g, par):
                wait(pool, s_pv, NS * (g - 1))
                v = values[:, :, :, :, :].rearrange("p c g t f -> p g c (t f)")[:, bass.ds(g, 1)]
                pool.tensor_copy(vg[par][:, :, :, 0:z.HD].rearrange("p (c t) h f -> p c (t h) f", c=z.NC),
                                 v.rearrange("p a c (n f) -> p (a c) n f", f=z.HD)).then_inc(s_vg, 1)

            def mask(g, step):
                pool.wait_ge(s_exp, 2 * (NS * g + step) + 2)
                pool.nop(nofuse=True)
                t = probs[step % RING][:, :, 0:P]
                pool.affine_select(out=t, in_=t, compare_op=ALU.is_ge, fill=0.0, base=0,
                                   pattern=[[0, HG], [1, P]], channel_multiplier=-1).then_inc(s_mask, 1)

            def body(it, first, last, b, k):
                for par in range(2):
                    g = 2 * it + par
                    for step in range(NS):
                        if step in MASKED:
                            mask(g, step)
                        if step == 3 and not (last and par == 1):
                            copy_v(g + 1, 1 - par)
                        if step == 4 and par == 1 and not first:
                            finish.divide(pool, it - 1, b, k)

            pool.sem_inc(finish.s_free, 1)
            copy_v(0, 0)
            for n, (whole, hi, lo) in enumerate(split):
                for k in range(z.DC):
                    pool.wait_ge(s_hi, n * z.DC + k + 1)
                    pool.tensor_tensor(lo[:, k], whole[:, k], hi[:, k].bitcast(F32),
                                       ALU.subtract).then_inc(s_lo, 1)
            pool.wait_ge(s_lo, 2 * z.DC)
            for n in range(2):
                pool.wait_ge(c["s_put"][n], z.CHUNKS * z.SG * 6 * 16)
            body(0, True, False, None, None)
            with pool.Fori(1, z.DC + 1) as it:
                body(it, False, False, 0, it - 1)
            with pool.Fori(z.DC + 1, ITERS - 1) as it:
                body(it, False, False, 1, it - 1 - z.DC)
            body(ITERS - 1, False, True, 1, z.DC - 2)

        @block.scalar
        def _(act):
            def exps(g, step, pair):
                n = NS * g + step
                w = z.CT - q0(step)
                wait(act, s_pv, n - RING + 1)
                act.wait_ge(s_qk, 2 * n + pair + 1)
                act.activation(probs[step % RING][:, 2 * pair:2 * pair + 2, 0:w], st[pair][:, :, 0:w],
                               ACT.Exp, scale=z.HD ** -0.5).then_inc(s_exp, 1)

            def evacuate(g, qc):
                act.wait_ge(s_pv, NS * g + (z.TT if qc == 0 else NS))
                wait(act, finish.s_bounce, 16 * g)
                act.copy(finish.raw[:, qc, :], po[:, :]).then_inc(finish.s_raw, 1)

            def load_rows(g, par, qc, last):
                act.wait_ge(s_taken, turned(g, qc, last))
                act.dma_start(qs[par][z.ROWS:z.ROWS + MP, qc], rows[qc][:, :]).then_inc(s_rows[qc], 16)

            def body(it, first, last):
                for par in range(2):
                    g = 2 * it + par
                    for step in range(NS):
                        if step == z.TT + LAG:
                            evacuate(g, 0)
                        exps(g, step, 0)
                        if step == LAG and not (first and par == 0):
                            evacuate(g - 1, 1)
                        exps(g, step, 1)
                        if step == 2:
                            load_rows(g, par, 1, last and par == 1)
                        if step == 6 and not (last and par == 1):
                            load_rows(g + 1, 1 - par, 0, False)

            for whole, hi, lo in split:
                for k in range(z.DC):
                    act.copy(hi[:, k], whole[:, k]).then_inc(s_hi, 1)
            load_rows(0, 0, 0, False)
            run(act, body)
            evacuate(z.G - 1, 1)

        @block.vector
        def _(dve):
            def negate(g, par, qc):
                base = 2 * (z.NC * g + (0 if qc == 0 else 1))
                m = top[:, par, qc].rearrange("p h t -> p (h t)")
                part = [neg[:, qc, n].rearrange("p h t -> p (h t)") for n in range(MP)]
                dve.tensor_scalar(part[0], m, -1.0, None, ALU.mult).then_inc(s_neg, 1)
                dve.wait_ge(s_neg, base + 1)
                dve.scalar_tensor_tensor(out=part[1], in0=m, scalar=-1.0, in1=part[0],
                                         op0=ALU.mult, op1=ALU.subtract).then_inc(s_neg, 1)

            def take(g, par, last, lo, hi, prologue=False):
                for k, n, (ahead, item) in ring(g, last, lo, hi):
                    if prologue and item == "turn 1":
                        continue
                    gi, pi = g + ahead, (par + ahead) % 2
                    dve.wait_ge(s_item, k + 1)
                    if item in ("turn 0", "turn 1"):
                        qc = int(item[-1])
                        wait(dve, s_rows[qc], 16 * gi)
                        dve.tensor_copy(rows[qc][:, :], pm[BANK[n]][0:MROWS, 0:P // 2].bitcast(BF16)).then_inc(s_taken, 1)
                        continue
                    qc, qt, kc, width, h, n_heads = item
                    to = (top2[:, pi] if kc < qc else top[:, pi, qc])[:, h:h + n_heads, qt]
                    dve.reduce_max(to, pm[BANK[n]][:, 0:n_heads * width].rearrange("p (h k) -> p h k", h=n_heads),
                                   AX.X).then_inc(s_taken, 2 if prologue and (k + 1) % NI == TURN[1] else 1)

            def after(g, par, hi):
                gi, pi = g + 1, 1 - par
                if hi == SLOTS[4]:
                    dve.wait_ge(s_taken, NI * gi + hi)
                    negate(gi, pi, 0)
                if hi == NI:
                    dve.wait_ge(s_taken, NI * gi + hi)
                    m = top[:, pi, 1].rearrange("p h t -> p (h t)")
                    dve.tensor_tensor(m, m, top2[:, pi].rearrange("p h t -> p (h t)"), ALU.max).then_inc(s_comb, 1)
                    dve.wait_ge(s_comb, gi + 1)
                    negate(gi, pi, 1)

            def body(it, first, last):
                for par in range(2):
                    g = 2 * it + par
                    end = last and par == 1
                    for step in range(NS):
                        take(g, par, end, SLOTS[step], SLOTS[step + 1])
                        if not end:
                            after(g, par, SLOTS[step + 1])
                        if step == 8 and not (first and par == 0):
                            finish.invert(dve, g - 1)

            dve.memset(ks[0][z.ROWS:, :, :, :], 1.0).then_inc(s_ones, 1)
            for step in range(NS):
                take(-1, 1, False, SLOTS[step], SLOTS[step + 1], prologue=True)
                after(-1, 1, SLOTS[step + 1])
            run(dve, body)

        @block.tensor
        def _(pe):
            def fill(g, par, last, lo, hi, prologue=False):
                for k, n, (ahead, item) in ring(g, last, lo, hi):
                    if prologue and item == "turn 1":
                        continue
                    gi, pi = g + ahead, (par + ahead) % 2
                    wait(pe, s_taken, emptied(k, n))
                    if item in ("turn 0", "turn 1"):
                        qc = int(item[-1])
                        pe.wait_ge(s_neg, 2 * (z.NC * gi + qc + 1))
                        pe.nop(nofuse=True)
                        pe.transpose(pm[BANK[n]][0:MROWS, 0:P // 2].bitcast(BF16),
                                     neg[:, qc].rearrange("p s h t -> p (s h t)"), c["ident_b"][:, :]).then_inc(s_item, 1)
                        continue
                    qc, qt, kc, width, h0, n_heads = item
                    for j in range(n_heads):
                        to = pm[BANK[n]][:, j * width:(j + 1) * width]
                        diagonal = kc == qc
                        mm = pe.matmul(to, qs[pi][0:z.ROWS, qc, h0 + j, qt * P:(qt + 1) * P],
                                       ks[pi][0:z.ROWS, kc, h0 + j, 0:width],
                                       start=(j == 0), stop=not diagonal, skip_group_check=True)
                        if diagonal:
                            mm = pe.matmul(to[:, width - P:], c["ident_b"][:, :], c["causal"][:, :],
                                           start=False, stop=True, skip_group_check=True)
                    mm.then_inc(s_item, 2 if prologue and (k + 1) % NI == TURN[1] else 1)

            def scores(g, par, step, pair):
                n = NS * g + step
                qc, kb = STEPS[step]
                if kb == 0 and pair == 0:
                    pe.wait_ge(s_rows[qc], 16 * (g + 1))
                wait(pe, s_exp, 2 * n + pair - 1)
                for h in (2 * pair, 2 * pair + 1):
                    mm = pe.matmul(st[pair][:, h % 2, 0:z.CT - q0(step)],
                                   ks[par][0:z.ROWS + MP, kb // z.TT, h, kb % z.TT * P:(kb % z.TT + 1) * P],
                                   qs[par][0:z.ROWS + MP, qc, h, q0(step):], start=True, stop=True)
                mm.then_inc(s_qk, 1)

            def weigh(g, par, step):
                n = NS * g + step
                qc, kb = STEPS[step]
                pe.wait_ge(s_exp, 2 * n + 2)
                if step in MASKED:
                    pe.wait_ge(s_mask, len(MASKED) * g + MASKED.index(step) + 1)
                if kb == 0:
                    wait(pe, finish.s_raw, 2 * g + qc)
                    if qc == 0:
                        pe.wait_ge(s_vg, g + 1)
                for h in range(HG):
                    mm = pe.matmul(po[32 * h:32 * h + 32, q0(step):], vg[par][:, kb, h, :],
                                   probs[step % RING][:, h, 0:z.CT - q0(step)],
                                   start=(kb == 0), stop=(kb == z.TT * (qc + 1) - 1))
                mm.then_inc(s_pv, 1)

            def loaded(eng_it, ahead, tc):
                pe.wait_ge(s_stack[ahead % 2][tc], 16 * LOADS * (eng_it + ahead // 2 + 1))

            def body(it, first, last):
                for par in range(2):
                    g = 2 * it + par
                    end = last and par == 1
                    for step in range(NS):
                        lo, hi = SLOTS[step], SLOTS[step + 1]
                        a, b, d = lo + (hi - lo + 3) // 4, lo + (hi - lo + 1) // 2, hi - (hi - lo) // 4
                        if step == 0 and not end:
                            loaded(it, par + 1, 0)
                        if step == z.TT and not end:
                            loaded(it, par + 1, 1)
                        scores(g, par, step, 0)
                        fill(g, par, end, lo, a)
                        scores(g, par, step, 1)
                        fill(g, par, end, a, d)
                        if step >= LAG:
                            weigh(g, par, step - LAG)
                        elif not (first and par == 0):
                            weigh(g - 1, 1 - par, NS - LAG + step)
                        fill(g, par, end, d, hi)

            loaded(0, 0, 0)
            for step in range(NS):
                if step == z.TT:
                    loaded(0, 0, 1)
                fill(-1, 1, False, SLOTS[step], SLOTS[step + 1], prologue=True)
            pe.wait_ge(s_ones, 2)
            run(pe, body)
            for step in range(NS - LAG, NS):
                weigh(z.G - 1, 1, step)



def ffn_phase(nc, z, c, residual, attn_t, finish, keys_t, wq_t, out):
    ER = EXPERTS * RANK // P
    NT = z.B * z.KT
    PAIRS = NT // 2
    BP = PAIRS // z.B
    with ExitStack() as ctx:
        def sb(name, shape, dt):
            return ctx.enter_context(nc.sbuf_tensor(name, shape, dt))

        def sem(name):
            return ctx.enter_context(nc.semaphore(name))

        def halves(name, shape):
            return sb(name + "_hi", shape, F32R), sb(name + "_lo", shape, F32R)

        res = residual_view(z, residual)
        x2t = attn_t
        up_hi, up_lo = halves("up_scaled", [P, ER, z.D])
        wf = [halves(f"w_ffn{b}", [P, z.DC, z.D]) for b in range(z.B)]
        a_hi, a_lo = halves("tile", [P, 2, z.DC, P])
        xn, ot = c["wo"][:, 0:2, :], c["wo"][:, 2:4, :]
        wsum = c["down"][:, 0:2, :]
        acc = c["down"][:, 2:4, :].rearrange("p a (k t) -> p (a k) t", k=2)
        stats = sb("stats2", [P, 2, 6], F32)
        mv = sb("mv2", [P, 2, 2], F32)
        small = sb("small2", [P, 4, 2], F32)
        total = sb("token_sums", [P, z.B, z.DC], F32)
        wq = sb("wq_gate", [P, z.DC, KEY], F32)
        keys = sb("keys", [KEY, EXPERTS], F32)
        gate_q = sb("gate_q", [KEY, z.B], F32)
        soft = sb("soft", [1, z.B, 3, EXPERTS], F32)
        ones = sb("ones", [1, P], F32)
        coeff = sb("coeff", [P, z.B, ER], F32)

        py = ctx.enter_context(nc.psum_tensor("py", [P, 2, z.D], F32))
        pt = ctx.enter_context(nc.psum_tensor("pt2", [P, 2, z.DC, P], F32))
        pw = ctx.enter_context(nc.psum_tensor("pw", [P, 2, z.D], F32))
        pg = ctx.enter_context(nc.psum_tensor("pg", [P, 2, z.D], F32))

        s_ones = sem("ones_set")
        s_keys = sem("gate_weights_loaded")
        s_ahi = sem("tile_hi_ready")
        s_alo = sem("tile_lo_ready")
        s_y = sem("product_ready")
        s_res = sem("residual_ready")
        s_ln = sem("ln2_steps")
        s_sqrt = sem("sqrt2_ready")
        s_xn = sem("xn2_ready")
        s_tr = sem("transposed2")
        s_xt = sem("x2t_ready")
        s_acc = sem("pair_summed")
        s_total = sem("token_sums_ready")
        s_gate = sem("gate_pe")
        s_gv = sem("gate_vector")
        s_ge = sem("gate_exp")
        s_uhi = sem("up_hi_ready")
        s_ulo = sem("up_lo_ready")
        s_eff = sem("w_ffn_summed_pe")
        s_sum = sem("w_ffn_with_base")
        s_whi = sem("w_ffn_hi_ready")
        s_wlo = sem("w_ffn_lo_ready")
        s_o = sem("out_tile_ready")
        s_out = [sem(f"out_stored{n}") for n in range(2)]

        LN_STEPS = 3 + 5
        GV = 7
        block = ctx.enter_context(nc.Block())

        def tile(t, n):
            return t[:, :, bass.ds(n * P, P)]

        def row_tile(n):
            return res[:, bass.ds(n, 1), :].rearrange("p a d -> p (a d)")

        @block.sync
        def _(sp):
            finish.rows_out(sp, z.G - 1)
            finish.rows_in(sp, z.G - 1, 1, z.G // 2 - 1)
            sp.dma_start(wq[:, :, :], wq_t.rearrange("(a p) n -> p a n", p=P)).then_inc(s_keys, 16)
            sp.dma_start(keys[:, :], keys_t).then_inc(s_keys, 16)
            finish.inverse_out(sp, z.G - 1)
            finish.inverse_in(sp, z.G - 1, 1)
            sp.wait_ge(finish.s_spread, 16 * z.G)
            dst = out.rearrange("b (t p) d -> (b t) p d", p=P)
            with sp.Fori(0, PAIRS) as m:
                for j in range(2):
                    sp.wait_ge(s_o, 2 * m + j + 1)
                    sp.nop(nofuse=True)
                    sp.dma_start(dst[bass.ds(2 * m + j, 1)].rearrange("a p d -> (a p) d"), ot[:, j, :]).then_inc(s_out[j], 16)
            for j in range(2):
                sp.wait_ge(s_out[j], PAIRS * 16)

        @block.gpsimd
        def _(pool):
            def lower(m, src):
                for j in range(2):
                    pool.wait_ge(s_ahi, 2 * m + j + 1)
                    pool.tensor_tensor(a_lo[:, j], tile(attn_t, 2 * src + j), a_hi[:, j].bitcast(F32),
                                       ALU.subtract).then_inc(s_alo, 1)

            def add_pair(m, first=False):
                both = x2t[:, :, bass.ds(2 * m * P, 2 * P)]
                pool.wait_ge(s_xt, 2 * m + 2)
                if first:
                    wait(pool, s_total, m // BP)
                    pool.tensor_copy(acc[:, :, :], both).then_inc(s_acc, 1)
                else:
                    pool.wait_ge(s_acc, m)
                    pool.tensor_tensor(acc[:, :, :], acc[:, :, :], both, ALU.add).then_inc(s_acc, 1)

            def weight_rest(b, k):
                n = b * z.DC + k
                pool.wait_ge(s_whi, n + 1)
                pool.tensor_tensor(wf[b][1][:, k], wsum[:, k % 2], wf[b][0][:, k].bitcast(F32), ALU.subtract).then_inc(s_wlo, 1)

            pool.memset(ones[:, :], 1.0).then_inc(s_ones, 1)
            lower(0, 0)
            lower(1, 1)
            lower(2, 2)
            add_pair(0, first=True)
            with pool.Fori(1, BP) as m:
                lower(m + 2, m + 2)
                add_pair(m)
            lower(BP + 2, BP + 2)
            add_pair(BP, first=True)
            lower(BP + 3, BP + 3)
            add_pair(BP + 1)
            lower(PAIRS, 0)
            add_pair(PAIRS - 2)
            for k in range(z.DC):
                weight_rest(0, k)
            add_pair(PAIRS - 1)
            with pool.Fori(1, BP) as m:
                lower(PAIRS + m, m)
            for k in range(z.DC):
                weight_rest(1, k)
            with pool.Fori(BP, PAIRS) as m:
                lower(PAIRS + m, m)

        @block.scalar
        def _(act):
            def upper(m, src, j):
                wait(act, s_y, 2 * m + j - 1)
                act.copy(a_hi[:, j], tile(attn_t, 2 * src + j)).then_inc(s_ahi, 1)

            def root(m):
                act.wait_ge(s_ln, LN_STEPS * m + 3)
                act.activation(small[:, 1], small[:, 0], ACT.Sqrt).then_inc(s_sqrt, 1)

            def keep(m):
                for j in range(2):
                    act.wait_ge(s_tr, 2 * m + j + 1)
                    act.copy(tile(x2t, 2 * m + j), pt[:, j]).then_inc(s_xt, 1)

            def both(m, src):
                for j in range(2):
                    upper(m, src, j)

            def first(m):
                root(m)
                both(m + 2, m + 2)
                keep(m)

            def exps(b):
                act.wait_ge(s_gv, GV * b + 3)
                act.activation(soft[:, b, 0], pg[0:1, 1, 0:EXPERTS], ACT.Exp, bias=soft[:, b, 1, 0:1],
                               scale=KEY ** -0.5, accum_out=soft[:, b, 1, 1:2]).then_inc(s_ge, 1)

            def scale_up(b):
                act.wait_ge(s_gv, GV * (b + 1))
                wait(act, s_eff, b * z.DC)
                for k in range(ER):
                    act.activation(up_hi[:, k], c["up"][:, k], ACT.Copy, scale=coeff[:, b, k:k + 1]).then_inc(s_uhi, 1)

            def weights(b):
                for k in range(z.DC):
                    act.wait_ge(s_sum, b * z.DC + k + 1)
                    act.copy(wf[b][0][:, k], wsum[:, k % 2]).then_inc(s_whi, 1)

            both(0, 0)
            both(1, 1)
            with act.Fori(0, 2) as m:
                first(m)
            act.wait_ge(finish.s_free, z.B * z.DC + 1)
            with act.Fori(2, BP + 1) as m:
                first(m)
            root(BP + 1)
            upper(PAIRS - 1, PAIRS - 1, 0)
            exps(0)
            upper(PAIRS - 1, PAIRS - 1, 1)
            keep(BP + 1)
            root(PAIRS - 2)
            scale_up(0)
            both(PAIRS, 0)
            keep(PAIRS - 2)
            root(PAIRS - 1)
            weights(0)
            keep(PAIRS - 1)
            both(PAIRS + 1, 1)
            upper(PAIRS + 2, 2, 0)
            exps(1)
            upper(PAIRS + 2, 2, 1)
            scale_up(1)
            both(PAIRS + 3, 3)
            weights(1)
            with act.Fori(BP, PAIRS) as m:
                both(PAIRS + m, m)

        @block.vector
        def _(dve):
            def ln(m):
                base = LN_STEPS * m
                for j in range(2):
                    row = row_tile(2 * m + j)
                    dve.wait_ge(s_y, 2 * m + j + 1)
                    dve.tensor_tensor(row, py[:, j, :], row, ALU.add).then_inc(s_res, 1)
                    dve.wait_ge(s_res, 2 * m + j + 1)
                    dve.nop(nofuse=True)
                    ins = dve.bn_stats(stats[:, j, :], row)
                ins.then_inc(s_ln, 1)
                dve.wait_ge(s_ln, base + 1)
                dve.nop(nofuse=True)
                for j in range(2):
                    ins = dve.bn_aggr(mv[:, j, :], stats[:, j, :])
                ins.then_inc(s_ln, 1)
                dve.wait_ge(s_ln, base + 2)
                dve.tensor_scalar(small[:, 0], mv[:, :, 1], EPS, None, ALU.add).then_inc(s_ln, 1)

            def normalize(m):
                rsqrt_newton(dve, [small[:, q] for q in range(4)], s_ln, LN_STEPS * m + 3, s_sqrt, m + 1)
                wait(dve, s_tr, 2 * m)
                for j in range(2):
                    dve.tensor_scalar(xn[:, j, :], row_tile(2 * m + j), mv[:, j, 0:1], small[:, 3, j:j + 1],
                                      ALU.subtract, ALU.mult).then_inc(s_xn, 1)

            def token_sums(b):
                dve.wait_ge(s_acc, BP * (b + 1))
                dve.reduce_sum(total[:, b], acc[:, :, :], AX.X).then_inc(s_total, 1)

            def gate_query(b):
                dve.wait_ge(s_gate, 3 * b + 1)
                dve.tensor_scalar(gate_q[:, b:b + 1], pg[:, 0, 0:1], 1.0 / z.S, None, ALU.mult).then_inc(s_gv, 1)

            def gate_max(b):
                dve.wait_ge(s_gate, 3 * b + 2)
                dve.reduce_max(soft[:, b, 1, 0:1], pg[0:1, 1, 0:EXPERTS], AX.X).then_inc(s_gv, 1)
                dve.wait_ge(s_gv, GV * b + 2)
                dve.tensor_scalar(soft[:, b, 1, 0:1], soft[:, b, 1, 0:1], -KEY ** -0.5, None, ALU.mult).then_inc(s_gv, 1)

            def gate_softmax(b):
                dve.wait_ge(s_ge, b + 1)
                dve.reciprocal(soft[:, b, 1, 2:3], soft[:, b, 1, 1:2]).then_inc(s_gv, 1)
                dve.wait_ge(s_gv, GV * b + 4)
                dve.tensor_scalar(soft[:, b, 2], soft[:, b, 0], soft[:, b, 1, 2:3], None, ALU.mult).then_inc(s_gv, 1)

            def scale_up(b):
                dve.wait_ge(s_gate, 3 * b + 3)
                spread = pg[:, 0, 0:EXPERTS].rearrange("p (k r) -> p k r", r=2)
                for half in range(2):
                    rows = slice(RANK * half, RANK * (half + 1))
                    dve.tensor_copy(coeff[rows, b, :], spread[rows, :, half]).then_inc(s_gv, 1)
                dve.wait_ge(s_gv, GV * (b + 1))
                for k in range(ER):
                    dve.wait_ge(s_uhi, b * ER + k + 1)
                    dve.scalar_tensor_tensor(out=up_lo[:, k], in0=c["up"][:, k], scalar=coeff[:, b, k:k + 1],
                                             in1=up_hi[:, k].bitcast(F32), op0=ALU.mult, op1=ALU.subtract).then_inc(s_ulo, 1)

            def weight(b, k):
                n = b * z.DC + k
                dve.wait_ge(s_eff, n + 1)
                wait(dve, s_wlo, n - 1)
                dve.tensor_tensor(wsum[:, k % 2], pw[:, k % 2, :], c["w_org"][:, k], ALU.add).then_inc(s_sum, 1)

            def result(m, j):
                dve.wait_ge(s_y, NT + 2 * m + j + 1)
                wait(dve, s_out[j], m * 16)
                dve.tensor_tensor(ot[:, j, :], py[:, j, :], row_tile(2 * m + j), ALU.add).then_inc(s_o, 1)

            dve.wait_ge(c["s_residual"], 16 * z.B)
            ln(0)
            finish.invert(dve, z.G - 1)
            normalize(0)
            ln(1)
            normalize(1)
            finish.divide(dve, z.B * z.DC - 1, z.B - 1, z.DC - 1)
            with dve.Fori(2, BP + 1) as m:
                ln(m)
                normalize(m)
            token_sums(0)
            ln(BP + 1)
            gate_query(0)
            normalize(BP + 1)
            gate_max(0)
            ln(BP + 2)
            gate_softmax(0)
            normalize(BP + 2)
            scale_up(0)
            ln(BP + 3)
            weight(0, 0)
            normalize(BP + 3)
            for k in range(1, z.DC):
                weight(0, k)
            result(0, 0)
            token_sums(1)
            result(0, 1)
            gate_query(1)
            result(1, 0)
            gate_max(1)
            result(1, 1)
            gate_softmax(1)
            scale_up(1)
            for j in range(2):
                result(2, j)
            for k in range(z.DC):
                weight(1, k)
            with dve.Fori(BP - 1, PAIRS) as m:
                for j in range(2):
                    result(m, j)

        @block.tensor
        def _(pe):
            wo = (c["wo_hi"], c["wo_lo"])
            down = (c["down_hi"], c["down_lo"])

            def product(m, j, w, w_ready=None):
                pe.wait_ge(s_alo, 2 * m + j + 1)
                for k in range(z.DC):
                    if w_ready is not None:
                        pe.wait_ge(s_wlo, w_ready + k + 1)
                    mm = exact_product(pe, py[:, j, :], a_hi[:, j, k], a_lo[:, j, k], w[0][:, k], w[1][:, k],
                                       k == 0, k == z.DC - 1)
                mm.then_inc(s_y, 1)

            def first(m, j):
                wait(pe, s_res, 2 * m + j - 1)
                product(m, j, wo)

            def last(m, j, b, w_ready=None):
                wait(pe, s_o, 2 * m + j - 1)
                product(PAIRS + m, j, wf[b], w_ready)

            def transposes(m):
                for j in range(2):
                    pe.wait_ge(s_xn, 2 * m + j + 1)
                    wait(pe, s_xt, 2 * m + j - 1)
                    for k in range(z.DC):
                        mm = pe.transpose(pt[:, j, k, :], xn[:, j, k * P:(k + 1) * P], c["ident"][:, :])
                    mm.then_inc(s_tr, 1)

            def gate_query(b):
                pe.wait_ge(s_ones, 1)
                pe.wait_ge(s_keys, 2 * 16)
                pe.wait_ge(s_total, b + 1)
                for k in range(z.DC):
                    mm = pe.matmul(pg[:, 0, 0:1], wq[:, k, :], total[:, b, k:k + 1], start=(k == 0), stop=(k == z.DC - 1))
                mm.then_inc(s_gate, 1)

            def gate_scores(b):
                pe.wait_ge(s_gv, GV * b + 1)
                pe.matmul(pg[0:1, 1, 0:EXPERTS], gate_q[:, b:b + 1], keys[:, :], start=True, stop=True).then_inc(s_gate, 1)

            def gate_spread(b):
                pe.wait_ge(s_gv, GV * b + 5)
                pe.matmul(pg[:, 0, 0:EXPERTS], ones[:, :], soft[:, b, 2], start=True, stop=True).then_inc(s_gate, 1)

            def weights(b):
                for k in range(z.DC):
                    wait(pe, s_sum, b * z.DC + k - 1)
                    for r in range(ER):
                        if k == 0:
                            pe.wait_ge(s_ulo, b * ER + r + 1)
                        cols = slice(k * P, (k + 1) * P)
                        mm = exact_product(pe, pw[:, k % 2, :], down[0][:, r, cols], down[1][:, r, cols],
                                           up_hi[:, r], up_lo[:, r], r == 0, r == ER - 1)
                    mm.then_inc(s_eff, 1)

            for j in range(2):
                first(0, j)
            for j in range(2):
                first(1, j)
            transposes(0)
            with pe.Fori(1, BP) as m:
                for j in range(2):
                    first(m + 1, j)
                transposes(m)
            for j in range(2):
                first(BP + 1, j)
            transposes(BP)
            gate_query(0)
            first(BP + 2, 0)
            gate_scores(0)
            first(BP + 2, 1)
            transposes(BP + 1)
            first(BP + 3, 0)
            gate_spread(0)
            first(BP + 3, 1)
            transposes(BP + 2)
            weights(0)
            transposes(BP + 3)
            pe.wait_ge(s_res, NT)
            last(0, 0, 0, w_ready=0)
            last(0, 1, 0)
            gate_query(1)
            last(1, 0, 0)
            gate_scores(1)
            last(1, 1, 0)
            last(2, 0, 0)
            gate_spread(1)
            last(2, 1, 0)
            weights(1)
            for j in range(2):
                last(3, j, 0)
            last(BP, 0, 1, w_ready=z.DC)
            last(BP, 1, 1)
            with pe.Fori(BP + 1, PAIRS) as m:
                for j in range(2):
                    last(m, j, 1)



def _rotation_tables(z):
    import numpy as np
    inv = (1.0 / np.float32(THETA) ** (np.arange(0, z.HD, 2, dtype=np.float32) / np.float32(z.HD))).astype(np.float32)
    angle = np.arange(z.S, dtype=np.float32)[:, None] * inv[None, :]
    both = np.stack([np.cos(angle), np.sin(angle)]).astype(np.float32)
    rows = np.tile(np.repeat(both.transpose(2, 0, 1), z.GH, axis=0), (4, 1, 1))
    chunks = rows.reshape(P, 2, z.NC, z.CT).transpose(2, 0, 1, 3)
    return np.ascontiguousarray(np.repeat(chunks, z.B, axis=0))


def kernel(L0_attn_hidden_states, L0_attn_wq, L0_attn_wk, L0_attn_wv, L0_attn_wo, L0_ffn_W_org,
           L0_ffn_lora_down, L0_ffn_lora_up, L0_ffn_lora_keys, L0_ffn_Wq):
    import numpy as np
    import concourse.bacc as bacc
    from concourse.bass_utils import run_bass_kernel_spmd

    x = np.asarray(L0_attn_hidden_states)
    z = Sizes(*x.shape)

    def by_half(w):
        w = np.asarray(w).reshape(z.D, z.SG, 4, z.GH, 2, z.HALF)
        return w.transpose(0, 1, 4, 2, 5, 3).reshape(z.D, z.D)

    arrays = {
        "x": x,
        "xc": x.reshape(z.B, z.NC, z.CT, z.D).transpose(1, 0, 2, 3).reshape(z.CHUNKS, z.CT, z.D),
        "w_in": np.concatenate([by_half(L0_attn_wq), by_half(L0_attn_wk), np.asarray(L0_attn_wv)], axis=1),
        "rope": _rotation_tables(z),
        "w_o": np.asarray(L0_attn_wo),
        "w_org_t": np.asarray(L0_ffn_W_org).T,
        "down_t": np.asarray(L0_ffn_lora_down).transpose(0, 2, 1).reshape(EXPERTS * RANK, z.D),
        "up": np.asarray(L0_ffn_lora_up).reshape(EXPERTS * RANK, z.D),
        "keys_t": np.asarray(L0_ffn_lora_keys).T,
        "wq_t": np.asarray(L0_ffn_Wq).T,
    }
    arrays = {n: np.ascontiguousarray(a) for n, a in arrays.items()}
    nc = bacc.Bacc("TRN2", target_bir_lowering=False, num_devices=1)
    args = [nc.dram_tensor("in_" + n, a.shape, mybir.dt.from_np(a.dtype), kind="ExternalInput").ap() for n, a in arrays.items()]
    args.append(nc.dram_tensor("y", x.shape, F32, kind="ExternalOutput").ap())
    layer_kernel(nc, *args)
    result = run_bass_kernel_spmd(nc, [{"in_" + n: a for n, a in arrays.items()}], core_ids=[0])
    return result.results[0]["y"]
```
